# Optimizing a Trainium2 kernel written in Bass

```python
import numpy as np
import jax
import jax.numpy as jnp

def _softmax(x, axis=-1):
    return jax.nn.softmax(x, axis=axis)
def _gelu(x):
    return jax.nn.gelu(x, approximate=True)
def _silu(x):
    return jax.nn.silu(x)
def _sigmoid(x):
    return jax.nn.sigmoid(x)
def _layernorm(x, axis=-1, eps=1e-5):
    m = jnp.mean(x, axis=axis, keepdims=True)
    v = jnp.var(x, axis=axis, keepdims=True)
    return (x - m) / jnp.sqrt(v + eps)
def _scatter_add(tgt, idx, src, axis=0):
    return tgt.at[idx].add(src)
def _segment_sum(src, seg, n):
    return jax.ops.segment_sum(src, seg, n)

kernel_name = 'mk_conv_preact_d4_conv_nchw16_449c52'

def setup_inputs(seed: int = 0):
    np.random.seed(seed)
    _w = jnp.asarray
    def _rec_inputs():
        import jax
        import jax.numpy as jnp
        _gk = jax.random.key(seed)
        x = -0.000125 + 0.9999 * jax.random.normal(jax.random.fold_in(_gk, 1), (8, 16, 512, 512), jnp.float32)
        return x
    x = _rec_inputs()
    def _L0_conv_setup():
        import jax, jax.numpy as jnp
        import numpy as np
        from jax import lax
        K = 3
        P = 1
        _CONV_PAD = K - 1 - P

        def _rconv(a, w):
            return lax.conv_general_dilated(a, w, window_strides=(1, 1), padding=[(_CONV_PAD, _CONV_PAD), (_CONV_PAD, _CONV_PAD)], dimension_numbers=('NCHW', 'OIHW', 'NCHW'))
        key = jax.random.key(seed)
        k1, k2, k3, k4, k5 = jax.random.split(key, 5)
        N, C_IN, C_OUT, H, W = (8, 16, 16, 512, 512)
        x = jax.random.normal(k1, (N, C_IN, H, W), dtype=jnp.float32)
        scale = 1.0 / np.sqrt(C_IN * K * K)
        w_real = jax.random.normal(k2, (C_IN, C_OUT, K, K), dtype=jnp.float32) * scale
        w_imag = jax.random.normal(k3, (C_IN, C_OUT, K, K), dtype=jnp.float32) * scale
        b_real = jax.random.normal(k4, (C_OUT,), dtype=jnp.float32) * scale
        b_imag = jax.random.normal(k5, (C_OUT,), dtype=jnp.float32) * scale
        return {'x': x, 'w_real': w_real, 'w_imag': w_imag, 'b_real': b_real, 'b_imag': b_imag}
    _L0_conv_all = _L0_conv_setup()
    _L0_conv_in = {k: v for k, v in _L0_conv_all.items() if k in ('w_real', 'w_imag', 'b_real', 'b_imag', )}
    del _L0_conv_all

    def _L1_conv_setup():
        import jax, jax.numpy as jnp
        import numpy as np
        key = jax.random.key(seed)
        uvs = jax.random.normal(key, (16, 16, 512, 256), dtype=jnp.float32)
        return {'uvs': uvs}
    _L1_conv_all = _L1_conv_setup()
    _L1_conv_in = {k: v for k, v in _L1_conv_all.items() if k in ()}
    del _L1_conv_all

    def _L2_conv_setup():
        import jax, jax.numpy as jnp
        import numpy as np
        B, CIN, COUT, H, W_ = (8, 16, 16, 1024, 1024)
        KH = KW = 3
        PH = PW = 1
        key = jax.random.key(seed)
        kx, kw = jax.random.split(key)
        x = jax.random.normal(kx, (B, CIN, H, W_), dtype=jnp.float32)
        Wt = jax.random.normal(kw, (COUT, CIN, KH, KW), dtype=jnp.float32) * 0.1
        return {'x': x, 'W': Wt}
    _L2_conv_all = _L2_conv_setup()
    _L2_conv_in = {k: v for k, v in _L2_conv_all.items() if k in ('W', )}
    del _L2_conv_all

    def _L3_conv_setup():
        import jax, jax.numpy as jnp
        import numpy as np
        from jax import lax
        C_OUT, C_IN, KH, KW = (16, 16, 3, 3)
        STRIDE = (1, 1)
        PADDING = ((1, 1), (1, 1))
        DILATION = (1, 1)
        key = jax.random.key(seed)
        kx, kw = jax.random.split(key)
        x = jax.random.normal(kx, (8, C_IN, 512, 512), dtype=jnp.float32)
        weight = jax.random.normal(kw, (C_OUT, C_IN * KH * KW), dtype=jnp.float32) * 0.1
        return {'x': x, 'weight': weight}
    _L3_conv_all = _L3_conv_setup()
    _L3_conv_in = {k: v for k, v in _L3_conv_all.items() if k in ('weight', )}
    del _L3_conv_all

    return {
        "x": x,
        "L0_conv_w_real": _L0_conv_in["w_real"],
        "L0_conv_w_imag": _L0_conv_in["w_imag"],
        "L0_conv_b_real": _L0_conv_in["b_real"],
        "L0_conv_b_imag": _L0_conv_in["b_imag"],
        "L2_conv_W": _L2_conv_in["W"],
        "L3_conv_weight": _L3_conv_in["weight"],
    }

def reference(x, L0_conv_w_real, L0_conv_w_imag, L0_conv_b_real, L0_conv_b_imag, L2_conv_W, L3_conv_weight):
    import jax
    import jax.numpy as jnp
    def _L0_conv_ref(x, w_real, w_imag, b_real, b_imag):
        import jax, jax.numpy as jnp
        import numpy as np
        from jax import lax
        K = 3
        P = 1
        _CONV_PAD = K - 1 - P

        def _rconv(a, w):
            return lax.conv_general_dilated(a, w, window_strides=(1, 1), padding=[(_CONV_PAD, _CONV_PAD), (_CONV_PAD, _CONV_PAD)], dimension_numbers=('NCHW', 'OIHW', 'NCHW'))
        X = jnp.fft.rfftn(x, axes=(-2, -1), norm='backward')
        Xr, Xi = (jnp.real(X), jnp.imag(X))
        wr = jnp.transpose(jnp.flip(w_real, axis=(-2, -1)), (1, 0, 2, 3))
        wi = jnp.transpose(jnp.flip(w_imag, axis=(-2, -1)), (1, 0, 2, 3))
        Yr = _rconv(Xr, wr) - _rconv(Xi, wi) + b_real[:, None, None]
        Yi = _rconv(Xr, wi) + _rconv(Xi, wr) + b_imag[:, None, None]
        Y = lax.complex(Yr, Yi)
        return jnp.fft.irfftn(Y, axes=(-2, -1), norm='backward')

    def _L1_conv_ref(uvs):
        import jax, jax.numpy as jnp
        import numpy as np
        u, v = jnp.split(uvs, 2, axis=1)
        left_gate = jax.nn.relu(jnp.sign(jnp.einsum('bkmd,bkd->bkm', u, v.sum(axis=2))))[..., None]
        right_gate = jax.nn.relu(jnp.sign(jnp.einsum('bknd,bkd->bkn', v, u.sum(axis=2))))[..., None]
        return jnp.concatenate([left_gate * u, right_gate * v], axis=1)

    def _L2_conv_ref(x, W):
        import jax, jax.numpy as jnp
        import numpy as np
        B, CIN, COUT, H, W_ = (8, 16, 16, 1024, 1024)
        KH = KW = 3
        PH = PW = 1
        return jax.lax.conv_general_dilated(x, W, window_strides=(1, 1), padding=((PH, PH), (PW, PW)), dimension_numbers=('NCHW', 'OIHW', 'NCHW'))

    def _L3_conv_ref(x, weight):
        import jax, jax.numpy as jnp
        import numpy as np
        from jax import lax
        C_OUT, C_IN, KH, KW = (16, 16, 3, 3)
        STRIDE = (1, 1)
        PADDING = ((1, 1), (1, 1))
        DILATION = (1, 1)
        w = weight.reshape(C_OUT, C_IN, KH, KW)
        out = lax.conv_general_dilated(x, w, window_strides=STRIDE, padding=PADDING, rhs_dilation=DILATION, dimension_numbers=('NCHW', 'OIHW', 'NCHW'), feature_group_count=1)
        return out

    def _gn(v, G=8, eps=1e-5):
        B_, C_, H_, W_ = v.shape
        g = v.reshape(B_, G, C_ // G, H_, W_)
        m = jnp.mean(g, axis=(2, 3, 4), keepdims=True)
        s = jnp.var(g, axis=(2, 3, 4), keepdims=True)
        return ((g - m) / jnp.sqrt(s + eps)).reshape(v.shape)

    def _ln_c(v, eps=1e-6):
        m = jnp.mean(v, axis=1, keepdims=True)
        s = jnp.var(v, axis=1, keepdims=True)
        return (v - m) / jnp.sqrt(s + eps)

    def _ln_t(v, eps=1e-5):
        m = jnp.mean(v, axis=-1, keepdims=True)
        s = jnp.var(v, axis=-1, keepdims=True)
        return (v - m) / jnp.sqrt(s + eps)

    def _to_tokens(v):
        B_, C_, H_, W_ = v.shape
        return v.reshape(B_, C_, H_ * W_).transpose(0, 2, 1)
    def _from_tokens(t, like):
        B_, C_, H_, W_ = like.shape
        return t.transpose(0, 2, 1).reshape(B_, C_, H_, W_)

    x = x + _L0_conv_ref(_gn(x), L0_conv_w_real, L0_conv_w_imag, L0_conv_b_real, L0_conv_b_imag)
    x = x + _L1_conv_ref(_gn(x))
    x = x + _L2_conv_ref(_gn(x), L2_conv_W)
    x = x + _L3_conv_ref(_gn(x), L3_conv_weight)
    return x


_drawn_inputs = setup_inputs


def setup_inputs(seed=0):
    import zlib

    import numpy as np

    out = dict(_drawn_inputs(seed))
    spreads = {}
    factors = {'L0_conv_b_real': 200.0, 'L0_conv_b_imag': 200.0}
    for name, (base, spread) in spreads.items():
        noise = np.random.default_rng([zlib.crc32(name.encode()), seed]).standard_normal(out[name].shape)
        drawn = base * np.exp(spread * noise) if base else spread * noise
        out[name] = jnp.asarray(drawn.astype(out[name].dtype))
    for name, factor in factors.items():
        out[name] = (out[name] * factor).astype(out[name].dtype)
    return out
```

```python
from contextlib import ExitStack

import numpy as np

import concourse.bass as bass
from concourse import mybir

F32 = mybir.dt.float32
ALU = mybir.AluOpType
ACT = mybir.ActivationFunctionType
AX_X = mybir.AxisListType.X

B, C, N = 8, 16, 512
P = 128
HP = P // 2
ROWS = 8
STRIPS = N // ROWS
UNROLL = 4
OUT_ROWS = 6
CO = C * OUT_ROWS
CONV_STRIPS = -(-N // OUT_ROWS)
EPS = 1e-5
HALF = N // 2
NG = 24
HW_ = HALF + NG
MIXED_CREDIT = 3
CONV_CREDIT = 4
A_CREDIT = 4
AXB, AXC, AXS = 0, 1, 2
ZR = 96
UR = 80
VMID, VTOP, VBOT = 0, 1, 2


def tables():
    n = np.arange(N)
    th = 2 * np.pi * n / N
    cos, sin = np.cos(th), np.sin(th)
    split = np.concatenate([n[::2], n[1::2]])
    t = n[None, :] - n[:, None]
    odd = t % 2 != 0
    hil = np.where(odd, (2.0 / N) / np.tan(np.where(odd, np.pi * t / N, 1.0)), 0.0)
    ev = (n % 2 == 0).astype(float)
    od = 1 - ev
    z = 0 * ev
    g_xc = [z, z, z, z, -ev * cos / N, -od * cos / N]
    g_hc = [z, z, 2 / N * od, 2 / N * ev, od * sin / N, ev * sin / N]
    g_xs = [z, z, z, z, -ev * sin / N, -od * sin / N]
    g_hs = [-2 / N * od, -2 / N * ev, z, z, -od * cos / N, -ev * cos / N]
    g = np.stack(g_xc + g_xs + g_hc + g_hs, 1)
    hil_t = np.zeros((P, 4, HW_))
    for k in range(4):
        rows = split[k * P:(k + 1) * P]
        cols = n[1::2] if k < 2 else n[::2]
        hil_t[:, k, :HALF] = hil[rows][:, cols]
        hil_t[:, k, HALF:] = g[rows]
    mean_fix = np.zeros((P, NG))
    mean_fix[:, 12 + 2:12 + 4] = -1.0
    mean_fix[:, 18:20] = 1.0
    trig_cols = np.broadcast_to(np.stack([cos[split], sin[split]]), (P, 2, N))

    p = np.arange(P)
    ch, r4, half = (p % HP) // 4, p % 4, p // HP
    strip = np.zeros((STRIPS, P, P + 4 + ZR))
    for s in range(STRIPS):
        row_out = ROWS * s + 4 * half + r4
        for k, f in enumerate((cos, sin, np.ones(N))):
            strip[s, 16 * k + ch, p] = f[row_out]
        strip[s, 64 + ch, p] = row_out == 0
        for gg in range(2):
            row = ROWS * s + 4 * gg + r4
            strip[s, :, P + 2 * gg] = cos[row]
            strip[s, :, P + 2 * gg + 1] = sin[row]
        row_in = ROWS * s + 4 * (1 - half) + r4
        for k, f in enumerate((np.ones(N), cos, sin)):
            strip[s, p, P + 4 + 32 * k + ch] = f[row_in] / N
    grp = ch // 2
    dst = [grp, (p // ROWS) // 2, np.arange(CO) // OUT_ROWS // 2]
    zc = np.arange(ZR) % 32
    dst.append(np.where(zc < C, zc // 2, -1))
    dst.append((grp + 4) % 8)
    scale = 1.0 / (2 * N * N)
    gsel = np.concatenate([(grp[:, None] == d[None, :]) * scale for d in dst], 1)
    go = np.arange(CO) // OUT_ROWS // 2
    csel = np.concatenate([(go[:, None] == d[None, :]) * scale for d in dst[1:3]], 1)
    partner = (ch[:, None] == (ch[None, :] + 8) % 16).astype(float)
    eye_mix = np.zeros((P, 2, 3, HP))
    for gg in range(2):
        for c in range(HP):
            eye_mix[HP * gg + c, gg, AXS, c] = 1.0
    eye_conv = np.zeros((P, 3, 3, CO))
    for v, off in ((VMID, 1), (VTOP, 0), (VBOT, 2)):
        for c in range(C):
            for r in range(OUT_ROWS):
                eye_conv[ROWS * c + r + off, v, 1, OUT_ROWS * c + r] = 1.0
    small = np.zeros((P, 2))
    small[:C, 0] = 1.0
    small[:CO, 1] = np.arange(CO) % OUT_ROWS >= OUT_ROWS - 2
    bias_rows = np.zeros((P, 2, N))
    bias_rows[64:64 + C, 0] = (split == 0)
    bias_rows[64:64 + C, 1] = -hil[0][split]
    f = lambda a: np.ascontiguousarray(a, dtype=np.float32)
    return {
        "t_eye": f(np.eye(P)), "t_hil": f(hil_t), "t_fix": f(mean_fix), "t_trig": f(trig_cols),
        "t_strip": f(strip), "t_gsel": f(gsel), "t_csel": f(csel), "t_partner": f(partner),
        "t_eye_mix": f(eye_mix), "t_eye_conv": f(eye_conv), "t_small": f(small), "t_bias": f(bias_rows),
    }


def placed(w_real, w_imag, b_real, b_imag, w2, w3):
    w = np.stack([w_real, w_imag])[:, :, :, ::-1, ::-1]
    w = w.transpose(1, 3, 4, 0, 2)
    mix = np.zeros((P, 3, 3, 2, HP), np.float32)
    uw = np.zeros((ZR, 3, 3, 2, C), np.float32)
    for c in range(C):
        for half in range(2):
            for r in range(4):
                mix[HP * half + 4 * c + r, :, :, :, r::4] = w[c]
        for k in range(3):
            uw[32 * k + c] = w[c]
    bias = np.zeros((P, 2), np.float32)
    bias[64:64 + C, 0] = b_real
    bias[64:64 + C, 1] = b_imag
    convs = []
    for wt in (w2, w3.reshape(C, C, 3, 3)):
        m = np.zeros((P, 3, 3, CO), np.float32)
        for v, off in ((VMID, 0), (VTOP, -1), (VBOT, 1)):
            for kh in range(3):
                for r in range(OUT_ROWS):
                    ri = r + kh + off
                    if 0 <= ri < ROWS:
                        for kw in range(3):
                            m[ri::ROWS, v, kw, r::OUT_ROWS] = wt[:, :, kh, kw].T
        convs.append(m)
    return {"w_mix": mix, "w_u": uw, "w_bias": bias, "w_conv": np.stack(convs)}


class Steps:

    def __init__(self, eng, sem, base):
        self.eng, self.sem, self.base, self.n = eng, sem, base, 0

    def did(self, ins):
        ins.then_inc(self.sem, 1)
        self.n += 1

    def settle(self):
        self.eng.wait_ge(self.sem, self.base + self.n)

    def then(self, ins):
        self.did(ins)
        self.settle()


DVE_B = 15
MOMENTS = 5
DVE_PREPS = 99


def program(nc, x, t_eye, t_hil, t_fix, t_trig, t_strip, t_gsel, t_csel, t_partner, t_eye_mix,
            t_eye_conv, t_small, t_bias, w_mix, w_u, w_bias, w_conv, out):
    with ExitStack() as ctx:
        def sb(name, *shape):
            return ctx.enter_context(nc.sbuf_tensor(name, list(shape), F32))

        def sem(name):
            return ctx.enter_context(nc.semaphore(name))

        in2 = nc.dram_tensor("in2", [C, N, N], F32).ap()
        in3 = nc.dram_tensor("in3", [C, N, N], F32).ap()

        ps = ctx.enter_context(nc.psum_tensor("ps", [P, 8, 512], F32))
        BT, BH, BP, BE, BM = 0, 1, 3, 6, 7

        eye = sb("eye", P, P)
        hil = sb("hil", P, 4, HW_)
        fix = sb("fix", P, NG)
        trig = sb("trig", P, 2, N)
        gsel = sb("gsel", P, 128 + 128 + CO + ZR + 128)
        csel = sb("csel", CO, 128 + CO)
        partner = sb("partner", P, P)
        small = sb("small", P, 2)
        bias_w = sb("bias_w", P, 2)
        mix_base = sb("mix_base", P, 3, 2, 3, HP)
        mix_s = sb("mix_s", P, 3, 2, 3, HP)
        eye_mix = sb("eye_mix", P, 2, 3, HP)
        u_base = sb("u_base", ZR, 6, 48)
        conv_s = sb("conv_s", P, 3, 3, CO)
        x1 = sb("x1", P, STRIPS, N)
        xin = sb("xin", P, UNROLL, N)
        strip = sb("strip", P, UNROLL, P + 4)
        tt = sb("tt", P, UNROLL, ZR)
        shared = sb("shared", P, UNROLL * (N + 2))
        stack = shared[:, 0:4 * N].rearrange("p (b g w) -> p b g w", b=2, g=2)
        cin = shared[:].rearrange("p (k w) -> p k w", k=UNROLL)
        xt = sb("xt", P, 4, P)
        wst = sb("wst", P, 2, 2, 3, HP)
        gp = sb("gp", P, 2, NG)
        gt = sb("gt", P, NG)
        gst = sb("gst", P, 2, 2, 12)
        ev_e = sb("ev_e", P, 2, 6)
        work = sb("work", P, 5, N)
        vc, vs, vy, junk, acc = (work[:, k, :] for k in range(5))
        colv = vs
        conv_w = work[:, 1:5, :].rearrange("p a b -> p (a b)")[:, 0:9 * CO]
        conv_eye = work[:, 1:5, :].rearrange("p a b -> p (a b)")[:, 9 * CO:18 * CO]
        u = sb("u", P, N)
        zt = sb("zt", P, 4, ZR)
        cols = sb("cols", P, 8, STRIPS + 24)
        vec = sb("vec", P, 32)
        red = sb("red", P, UNROLL)
        cout = sb("cout", CO, 2, N)

        s_const = sem("constants_loaded")
        s_setup = sem("setup_steps")
        s_based = sem("setup_done")
        s_pool = sem("pool_zeroed")
        a_loaded = [sem(f"a_loaded{k}") for k in range(UNROLL)]
        a_squared, a_summed, a_projected = sem("a_squared"), sem("a_summed"), sem("a_projected")
        d_prep, v_var, a_root = sem("dve_prep_steps"), sem("var_ready"), sem("root_ready")
        p_stat, p_zt, p_zin, p_zh, p_u = sem("pe_stat"), sem("pe_zt"), sem("pe_zin"), sem("pe_zh"), sem("pe_u")
        v_sums0, v_zt, v_scaled, v_z, v_u = sem("sums0"), sem("zt_ready"), sem("mix_scaled"), sem("z_ready"), sem("u_ready")
        x_loaded = [sem(f"x_loaded{k}") for k in range(UNROLL)]
        turned, xt_ready, h_done, h_ready = sem("turned"), sem("xt_ready"), sem("h_done"), sem("h_ready")
        g_taken, g_ready, w_ready, e_done = sem("g_taken"), sem("g_ready"), sem("w_ready"), sem("e_done")
        pc_done, ps_done, mixed = sem("pc_done"), sem("ps_done"), sem("mixed")
        b_steps, y_done, y_squared, y_added = sem("b_steps"), sem("y_done"), sem("y_squared"), sem("y_added")
        acc_zero = sem("acc_zeroed")
        v_sums1, p_stat1, v_colv = sem("sums1"), sem("pe_stat1"), sem("colv_ready")
        dotted = sem("dotted")
        v_sums2, p_stat2, v_conv2 = sem("sums2"), sem("pe_stat2"), sem("conv2_weights")
        gated, in2_stored = sem("gated"), sem("in2_stored")
        c_loaded = [sem(f"c_loaded{k}") for k in range(UNROLL)]
        c_stored = [sem(f"c_stored{k}") for k in range(2)]
        cw_loaded = sem("conv_weights_loaded")
        convolved, evicted, c_squared, c_reduced = sem("convolved"), sem("evicted"), sem("c_squared"), sem("c_reduced")
        v_sums3, p_stat3, v_conv3, p_bias3, v_bias3 = sem("sums3"), sem("pe_stat3"), sem("conv3_weights"), sem("pe_bias3"), sem("bias3")

        block = ctx.enter_context(nc.Block())

        MEAN, RS, NEGM, VAR, MZ, MEANP, SV, BIAS3 = 0, 1, 2, 3, 5, 6, 7, 9
        ST, ST1, CM, ZV = 12, 14, 16, 20

        def v1(k, p0=0, p1=P):
            return vec[p0:p1, k:k + 1]

        USES = [len(range(k, CONV_STRIPS, UNROLL)) for k in range(UNROLL)]
        MIDS = CONV_STRIPS - 2
        assert MIDS % UNROLL == 0 and STRIPS % UNROLL == 0

        def conv_strips(eng, emit):
            emit(0, 0, 0, VTOP)
            with eng.Fori(0, MIDS // UNROLL) as j:
                for k in range(UNROLL):
                    v = 1 + k
                    emit(j * UNROLL + v, v % UNROLL, j + v // UNROLL, VMID)
            v = CONV_STRIPS - 1
            emit(v, v % UNROLL, v // UNROLL, VBOT)

        G_OUT, G_CIN, G_CO = (0, 128), (128, 256), (256, 256 + CO)
        G_Z = (256 + CO, 256 + CO + ZR)
        G_PART = (256 + CO + ZR, 256 + CO + ZR + 128)

        split_in = lambda a: a.rearrange("p (w q) -> p q w", q=2)
        halves = lambda a: a.rearrange("p (q w) -> p q w", q=2)

        @block.sync
        def _(sp):
            for dst, src in ((eye[:], t_eye), (hil[:], t_hil), (fix[:], t_fix), (trig[:], t_trig),
                             (gsel[:], t_gsel), (csel[:], t_csel), (partner[:], t_partner),
                             (small[:], t_small), (bias_w[:], w_bias), (eye_mix[:], t_eye_mix),
                             (x1[:, 0:3, :].rearrange("p a b -> p (a b)")[:, 0:1152], w_mix.rearrange("p a b c d -> p (a b c d)")),
                             (x1[0:ZR, 3:4, 0:288].rearrange("p a b -> p (a b)"), w_u.rearrange("p a b c d -> p (a b c d)")),
                             (x1[:, 4:6, :], t_bias)):
                sp.dma_start(dst, src).then_inc(s_const, 16)

            def load_x(i, s, slot, dst, loaded):
                for g in range(2):
                    src = x[i].rearrange("c (s g r) w -> s g c r w", g=2, r=4)[s, g]
                    sp.dma_start(dst[HP * (1 - g):HP * (2 - g), slot, :], src).then_inc(loaded[slot], 16)

            with sp.Fori(0, B) as i:
                with sp.Fori(0, STRIPS // UNROLL) as j:
                    for k in range(UNROLL):
                        s = j * UNROLL + k
                        t = i * STRIPS + s
                        sp.wait_ge(a_squared, t + 1)
                        sp.wait_ge(a_summed, t + 1)
                        sp.wait_ge(a_projected, t + 1)
                        load_x(i, s, k, xin, a_loaded)
                        sp.dma_start(tt[:, k, :], t_strip[s][:, P + 4:P + 4 + ZR]).then_inc(a_loaded[k], 16)
                with sp.Fori(0, STRIPS // UNROLL) as j:
                    for k in range(UNROLL):
                        s = j * UNROLL + k
                        t = i * STRIPS + s
                        sp.wait_ge(a_squared, i * STRIPS + STRIPS + A_CREDIT)
                        sp.wait_ge(a_summed, i * STRIPS + STRIPS + A_CREDIT)
                        sp.wait_ge(a_projected, i * STRIPS + STRIPS + A_CREDIT)
                        sp.wait_ge(mixed, t + 1 - UNROLL + MIXED_CREDIT)
                        load_x(i, s, k, xin, x_loaded)
                        sp.dma_start(strip[:, k, :], t_strip[s][:, 0:P + 4]).then_inc(x_loaded[k], 16)
                sp.wait_ge(v_sums2, i + 1)
                sp.dma_start(conv_w, w_conv[0].rearrange("p a b c -> p (a b c)")).then_inc(cw_loaded, 16)
                sp.dma_start(conv_eye, t_eye_conv.rearrange("p a b c -> p (a b c)")).then_inc(cw_loaded, 16)
                with sp.Fori(0, STRIPS // UNROLL) as j:
                    sp.wait_ge(gated, i * STRIPS + (j + 1) * UNROLL)
                    for g in range(2):
                        dst = in2.rearrange("c (s g r) w -> s g c r w", g=2, r=4)
                        for k in range(UNROLL):
                            s = j * UNROLL + k
                            sp.dma_start(dst[s, g], x1[HP * g:HP * g + HP, bass.ds(s, 1), :]).then_inc(in2_stored, 16)
                sp.wait_ge(v_conv2, i + 1)
                sp.dma_start(conv_w, w_conv[1].rearrange("p a b c -> p (a b c)")).then_inc(cw_loaded, 16)
                for ph, src in ((0, in2), (1, in3)):
                    if ph == 0:
                        sp.wait_ge(in2_stored, (i + 1) * (STRIPS * 32))
                    else:
                        for k in range(2):
                            sp.wait_ge(c_stored[k], (i * 2 + 1) * (8 * CONV_STRIPS))
                    sp.wait_ge(v_conv2 if ph == 0 else v_conv3, i + 1)

                    def load(v, slot, use, variant):
                        r0 = 0 if variant == VTOP else N - ROWS if variant == VBOT else sp.snap(v * OUT_ROWS - 1)
                        sp.wait_ge(convolved, (i * 2 + ph) * CONV_STRIPS + v + 1 - UNROLL + CONV_CREDIT)
                        sp.dma_start(cin[:, slot, 1:N + 1], src[:, bass.ds(r0, ROWS), :]).then_inc(c_loaded[slot], 16)

                    conv_strips(sp, load)
            for k in range(2):
                sp.wait_ge(c_stored[k], B * 2 * 8 * CONV_STRIPS)

        @block.gpsimd
        def _(pool):
            nc.gpsimd.memset(u[:], 0.0).then_inc(s_pool, 1)
            nc.gpsimd.memset(u_base[:], 0.0).then_inc(s_pool, 1)
            with pool.Fori(0, B) as i:
                with pool.Fori(0, STRIPS) as s:
                    t = i * STRIPS + s
                    pool.wait_ge(acc_zero, i + 1)
                    pool.wait_ge(y_done, t + 1)
                    pool.wait_ge(y_added, t)
                    nc.gpsimd.tensor_tensor(acc, acc, x1[:, bass.ds(s, 1), :].rearrange("p a w -> p (a w)"), ALU.add).then_inc(y_added, 1)

        @block.scalar
        def _(act):
            act.sem_inc(a_squared, A_CREDIT)
            act.sem_inc(evicted, CONV_CREDIT)
            with act.Fori(0, B) as i:
                with act.Fori(0, STRIPS // UNROLL) as j:
                    for k in range(UNROLL):
                        s = j * UNROLL + k
                        t = i * STRIPS + s
                        act.wait_ge(a_loaded[k], (i * (STRIPS // UNROLL) + j + 1) * 48)
                        act.wait_ge(a_squared, t + A_CREDIT)
                        nc.scalar.activation(junk, xin[:, k, :], ACT.Square,
                                             accum_out=cols[:, 1, bass.ds(s, 1)]).then_inc(a_squared, 1)
                def root(n, dst, p1=P):
                    act.wait_ge(v_var, i * MOMENTS + n + 1)
                    nc.scalar.activation(v1(dst + 1, 0, p1), v1(dst + 3, 0, p1), ACT.Sqrt).then_inc(a_root, 1)

                root(0, 0)
                root(1, ZV, ZR)
                act.wait_ge(v_scaled, i + 1)

                def bring(t, loads, k):
                    act.wait_ge(x_loaded[k], loads * 48)
                    act.wait_ge(mixed, t - 1 + MIXED_CREDIT)
                    b = k % 2
                    nc.scalar.activation(halves(stack[0:HP, b, 0, :]), split_in(xin[HP:P, k, :]), ACT.Identity,
                                         bias=v1(NEGM, HP, P))
                    nc.scalar.activation(halves(stack[HP:P, b, 1, :]), split_in(xin[0:HP, k, :]), ACT.Identity,
                                         bias=v1(NEGM, 0, HP))
                    act.wait_ge(turned, t + 1)
                    act.wait_ge(h_done, t)
                    nc.scalar.activation(xt[:].rearrange("p a b -> p (a b)"), ps[:, BT, :], ACT.Identity).then_inc(xt_ready, 1)
                    act.wait_ge(h_done, t + 1)
                    act.wait_ge(g_ready, t)
                    nc.scalar.activation(gp[:], ps[:, BH:BH + 2, HALF:HW_], ACT.Identity).then_inc(g_taken, 1)
                    nc.scalar.activation(halves(stack[HP:P, b, 0, :]), ps[HP:P, BH:BH + 2, 0:HALF], ACT.Identity).then_inc(h_ready, 1)
                    nc.scalar.activation(halves(stack[0:HP, b, 1, :]), ps[0:HP, BH:BH + 2, 0:HALF], ACT.Identity).then_inc(h_ready, 1)

                def square(t, s):
                    act.wait_ge(y_done, t + 1)
                    act.wait_ge(y_squared, t)
                    nc.scalar.activation(junk, x1[:, bass.ds(s, 1), :].rearrange("p a w -> p (a w)"), ACT.Square,
                                         accum_out=cols[:, 1, bass.ds(s, 1)]).then_inc(y_squared, 1)

                u0 = i * (STRIPS // UNROLL)
                t0 = i * STRIPS
                bring(t0, u0 + 1, 0)
                with act.Fori(0, STRIPS // UNROLL - 1) as j:
                    for k in range(UNROLL):
                        s = j * UNROLL + k
                        bring(t0 + s + 1, u0 + j + 1 + (k + 1) // UNROLL, (k + 1) % UNROLL)
                        square(t0 + s, s)
                for s in range(STRIPS - UNROLL, STRIPS):
                    if s + 1 < STRIPS:
                        bring(t0 + s + 1, u0 + s // UNROLL + 1, (s + 1) % UNROLL)
                    square(t0 + s, s)

                root(2, 0)
                root(3, ZV)
                for ph in range(2):
                    if ph == 1:
                        root(4, ZV)
                    act.wait_ge(v_conv2 if ph == 0 else v_bias3, i + 1 if ph == 0 else i * 3 + 3)

                    def evict(v, slot, use, variant):
                        n = (i * 2 + ph) * CONV_STRIPS + v
                        act.wait_ge(convolved, n + 1 + CONV_CREDIT)
                        o = slot % 2
                        act.wait_ge(c_stored[o], (i * 2 + ph) * (8 * CONV_STRIPS) + (use * 2 + slot // 2) * 16)
                        if ph == 0:
                            act.wait_ge(c_squared, i * CONV_STRIPS + v - 1 + CONV_CREDIT)
                            nc.scalar.activation(cout[:, o, :], ps[0:CO, 2 + slot, :], ACT.Identity, bias=v1(CM, 0, CO),
                                                 accum_out=cols[0:CO, 2, bass.ds(v, 1)]).then_inc(evicted, 1)
                        else:
                            nc.scalar.activation(cout[:, o, :], ps[0:CO, 2 + slot, :], ACT.Identity,
                                                 bias=v1(BIAS3 + variant, 0, CO)).then_inc(evicted, 1)
                        act.wait_ge(evicted, n + 1 + CONV_CREDIT)
                        dst = in3 if ph == 0 else out[i]
                        r0 = v * OUT_ROWS
                        if variant == VBOT:
                            act.wait_ge(c_stored[1 - o], (i * 2 + ph + 1) * (8 * CONV_STRIPS))
                            r0 = N - OUT_ROWS
                        act.dma_start(dst[:, bass.ds(r0, OUT_ROWS), :], cout[:, o, :]).then_inc(c_stored[o], 16)

                    conv_strips(act, evict)

        @block.vector
        def _(dve):
            V = nc.vector
            dve.sem_inc(a_summed, A_CREDIT)
            dve.sem_inc(c_squared, CONV_CREDIT)
            st = Steps(dve, s_setup, 0)
            dve.wait_ge(s_const, 13 * 16)
            dve.wait_ge(s_pool, 2)
            wm = x1[:, 0:3, :].rearrange("p a b -> p (a b)")[:, 0:1152].rearrange("p (a b c d) -> p a b c d", a=3, b=3, c=2)
            wu = x1[0:ZR, 3:4, 0:288].rearrange("p a b -> p (a b)").rearrange("p (a b c d) -> p a b c d", a=3, b=3, c=2)
            tmp = x1[:, 8:16, :].rearrange("p a b -> p (a b)")
            q3 = tmp[:, 0:1152].rearrange("p (j b c d) -> p j b c d", j=3, b=3, c=2)
            pm = tmp[:, 1152:1152 + 768].rearrange("p (j f c d) -> p j f c d", j=3, f=2, c=2)
            fl = lambda a: a.rearrange("p b c d -> p (b c d)")
            st.did(V.tensor_copy(fl(q3[:, 0]), fl(wm[:, 1])))
            st.did(V.tensor_tensor(fl(q3[:, 1]), fl(wm[:, 2]), fl(wm[:, 0]), ALU.add))
            st.then(V.tensor_tensor(fl(q3[:, 2]), fl(wm[:, 2]), fl(wm[:, 0]), ALU.subtract))
            for j in range(3):
                for f, op in enumerate((ALU.add, ALU.subtract)):
                    st.did(V.tensor_tensor(pm[:, j, f], q3[:, j, 2], q3[:, j, 0], op))
            st.settle()
            for j in range(3):
                re, im = ((1, 0), (1, 1)) if j < 2 else ((1, 1), (-1, 0))
                for g in range(2):
                    for kind in range(2):
                        h0 = HP * (g ^ kind)
                        sl = slice(h0, h0 + HP)
                        for a in range(3):
                            which, sgn = ((re, 1), (im, -1)) [kind] if a != AXC else ((im, 1), (re, 1))[kind]
                            src = q3[sl, j, 1, which[1]] if a == AXS else pm[sl, j, a, which[1]]
                            st.did(V.tensor_scalar(mix_base[sl, j, g, a, :], src, float(which[0] * sgn), None, ALU.mult))
            pu = tmp[0:ZR, 2048:2048 + 192].rearrange("p (k f c d) -> p k f c d", k=3, f=2, c=2)
            for d1 in (0, 2):
                for f, op in enumerate((ALU.add, ALU.subtract)):
                    st.did(V.tensor_tensor(pu[:, d1, f], wu[:, d1, 2], wu[:, d1, 0], op))
            st.settle()
            for z, blk, d1, re, im in ((0, 0, 2, (1, 0), (1, 1)), (0, 1, 2, (1, 1), (-1, 0)),
                                       (1, 2, 0, (1, 0), (1, 1)), (2, 2, 0, (-1, 1), (1, 0))):
                sl = slice(32 * z, 32 * z + C)
                for k, (which, sgn, f) in enumerate(((re, 1, 0), (im, -1, 0), (im, 1, 1), (re, 1, 1), (re, 1, 2), (im, -1, 2))):
                    src = wu[sl, d1, 1, which[1]] if f == 2 else pu[sl, d1, f, which[1]]
                    st.did(V.tensor_scalar(u_base[sl, k, 16 * blk:16 * blk + 16], src, float(-which[0] * sgn), None, ALU.mult))
            sl = slice(64, 64 + C)
            br = x1[:, 4:6, :]
            st.then(V.tensor_scalar(u[sl, :], br[sl, 0, :], bias_w[sl, 0:1], None, ALU.mult))
            V.scalar_tensor_tensor(u[sl, :], br[sl, 1, :], bias_w[sl, 1:2], u[sl, :], ALU.mult, ALU.add).then_inc(s_based, 1)
            dve.wait_ge(s_based, 1)

            def moments(c, n, src, dst, p1=P):
                mean, rs, neg, var, t = (v1(dst + k, 0, p1) for k in (0, 1, 2, 3, 4))
                c.then(V.tensor_copy(vec[0:p1, dst:dst + 2], src))
                c.did(V.tensor_scalar(neg, mean, -1.0, None, ALU.mult))
                c.then(V.tensor_tensor(var, mean, mean, ALU.mult))
                c.then(V.tensor_tensor(var, rs, var, ALU.subtract))
                V.tensor_scalar(var, var, 0.0, EPS, ALU.max, ALU.add).then_inc(v_var, 1)
                dve.wait_ge(a_root, i * MOMENTS + n + 1)
                c.then(V.reciprocal(rs, rs))
                c.then(V.tensor_tensor(t, rs, rs, ALU.mult))
                c.then(V.tensor_tensor(t, t, var, ALU.mult))
                c.then(V.tensor_scalar(t, t, -0.5, 1.5, ALU.mult, ALU.add))
                c.then(V.tensor_tensor(rs, rs, t, ALU.mult))

            with dve.Fori(0, B) as i:
                c = Steps(dve, d_prep, i * DVE_PREPS)
                dve.wait_ge(v_conv3, i)
                V.memset(acc, 0.0).then_inc(acc_zero, 1)
                with dve.Fori(0, STRIPS // UNROLL) as j:
                    for k in range(UNROLL):
                        s = j * UNROLL + k
                        dve.wait_ge(a_loaded[k], (i * (STRIPS // UNROLL) + j + 1) * 48)
                        V.tensor_reduce(cols[:, 0, bass.ds(s, 1)], xin[:, k, :], AX_X, ALU.add).then_inc(a_summed, 1)
                dve.wait_ge(a_summed, i * STRIPS + STRIPS + A_CREDIT)
                dve.wait_ge(a_squared, i * STRIPS + STRIPS + A_CREDIT)
                for q in range(2):
                    c.did(V.tensor_reduce(v1(ST + q), cols[:, q, 0:STRIPS], AX_X, ALU.add))
                c.settle()
                V.tensor_copy(vec[:, ST1:ST1 + 2], vec[:, ST:ST + 2]).then_inc(v_sums0, 1)
                dve.wait_ge(a_projected, i * STRIPS + STRIPS + A_CREDIT)
                V.tensor_copy(zt[:], ps[:, 2:6, 0:ZR]).then_inc(v_zt, 1)
                dve.wait_ge(p_stat, i + 1)
                moments(c, 0, ps[:, BM, 0:2], 0)
                moments(c, 1, ps[0:ZR, BM, 2:4], ZV, ZR)
                c.then(V.tensor_tensor(v1(MZ, 0, ZR), v1(ZV, 0, ZR), small[0:ZR, 0:1], ALU.mult))
                flat = lambda a: a.rearrange("p g a o -> p (g a o)")
                for jj in (1, 2):
                    c.did(V.tensor_scalar(flat(mix_s[:, jj]), flat(mix_base[:, jj]), v1(1), None, ALU.mult))
                V.scalar_tensor_tensor(flat(mix_s[:, 0]), flat(mix_base[:, 0]), v1(1), flat(eye_mix[:]), ALU.mult, ALU.add).then_inc(v_scaled, 1)
                dve.wait_ge(v_scaled, i + 1)
                zs, zhs, zg = vc, vs, gt
                dve.wait_ge(p_zin, i + 1)
                c.did(V.tensor_scalar(zs[0:ZR, :], ps[0:ZR, BT, :], v1(MZ, 0, ZR), v1(ZV + 1, 0, ZR), ALU.subtract, ALU.mult))
                dve.wait_ge(p_zh, i + 1)
                c.did(V.tensor_scalar(halves(zhs[0:ZR, :]), ps[0:ZR, BH:BH + 2, 0:HALF], v1(ZV + 1, 0, ZR), None, ALU.mult))
                c.then(V.scalar_tensor_tensor(zg[0:ZR, :], fix[0:ZR, :], v1(MZ, 0, ZR), ps[0:ZR, BH, HALF:HW_], ALU.mult, ALU.add))
                c.then(V.tensor_tensor(zg[0:ZR, :], zg[0:ZR, :], ps[0:ZR, BH + 1, HALF:HW_], ALU.add))
                V.tensor_scalar(zg[0:ZR, :], zg[0:ZR, :], v1(ZV + 1, 0, ZR), None, ALU.mult).then_inc(v_z, 1)
                dve.wait_ge(p_u, i + 1)
                c.then(V.tensor_copy(ev_e[0:48, 0, :], ps[0:48, BE, 0:6]))
                for q in range(2):
                    w = slice(HALF * q, HALF * (q + 1))
                    c.did(V.scalar_tensor_tensor(vy[0:48, w], ps[0:48, BP + AXB, w], ev_e[0:48, 0, q:q + 1], trig[0:48, 0, w], ALU.add, ALU.mult))
                    c.did(V.scalar_tensor_tensor(u[0:48, w], ps[0:48, BP + AXC, w], ev_e[0:48, 0, 2 + q:3 + q], trig[0:48, 1, w], ALU.add, ALU.mult))
                c.settle()
                c.then(V.tensor_tensor(vy[0:48, :], vy[0:48, :], u[0:48, :], ALU.add))
                for q in range(2):
                    w = slice(HALF * q, HALF * (q + 1))
                    V.scalar_tensor_tensor(u[0:48, w], ps[0:48, BP + AXS, w], ev_e[0:48, 0, 4 + q:5 + q], vy[0:48, w], ALU.add, ALU.add).then_inc(v_u, 1)
                dve.wait_ge(v_u, i * 2 + 2)

                t0 = i * STRIPS

                def build(b, k, loads, t):
                    dve.wait_ge(x_loaded[k], loads * 48)
                    dve.wait_ge(mixed, t - 1 + MIXED_CREDIT)
                    fg = lambda a: a.rearrange("p a o -> p (a o)")
                    for g in range(2):
                        b.did(V.scalar_tensor_tensor(fg(wst[:, k % 2, g]), fg(mix_s[:, 1, g]), strip[:, k, P + 2 * g:P + 2 * g + 1], fg(mix_s[:, 0, g]), ALU.mult, ALU.add))
                    b.settle()
                    b.did(V.scalar_tensor_tensor(fg(wst[:, k % 2, 0]), fg(mix_s[:, 2, 0]), strip[:, k, P + 1:P + 2], fg(wst[:, k % 2, 0]), ALU.mult, ALU.add))
                    V.scalar_tensor_tensor(fg(wst[:, k % 2, 1]), fg(mix_s[:, 2, 1]), strip[:, k, P + 3:P + 4], fg(wst[:, k % 2, 1]), ALU.mult, ALU.add).then_inc(w_ready, 1)

                def row_sums(b, k, t):
                    dve.wait_ge(g_taken, t + 1)
                    dve.wait_ge(g_ready, t)
                    b.then(V.scalar_tensor_tensor(gt[:], fix[:], v1(0), gp[:, 0, :], ALU.mult, ALU.add))
                    o = k % 2
                    gx, gh = slice(0, 12), slice(12, 24)
                    b.did(V.tensor_tensor(gst[0:HP, o, 0, :], gt[HP:P, gx], gp[HP:P, 1, gx], ALU.add))
                    b.did(V.tensor_tensor(gst[HP:P, o, 0, :], gt[HP:P, gh], gp[HP:P, 1, gh], ALU.add))
                    b.did(V.tensor_tensor(gst[0:HP, o, 1, :], gt[0:HP, gh], gp[0:HP, 1, gh], ALU.add))
                    V.tensor_tensor(gst[HP:P, o, 1, :], gt[0:HP, gx], gp[0:HP, 1, gx], ALU.add).then_inc(g_ready, 1)

                def combine(b, k, s, t):
                    o = k % 2
                    dve.wait_ge(e_done, t + 1)
                    b.then(V.tensor_copy(ev_e[:, o, :], ps[:, BE, 0:6]))
                    dve.wait_ge(y_done, t)
                    for a, done, dst in ((AXB, pc_done, vc), (AXC, ps_done, vs)):
                        dve.wait_ge(done, t + 1)
                        for q in range(2):
                            w = slice(HALF * q, HALF * (q + 1))
                            b.did(V.scalar_tensor_tensor(dst[:, w], ps[:, BP + a, w], ev_e[:, o, 2 * a + q:2 * a + q + 1], trig[:, a, w], ALU.add, ALU.mult))
                    b.settle()
                    dve.wait_ge(mixed, t + 1 + MIXED_CREDIT)
                    for q in range(2):
                        w = slice(HALF * q, HALF * (q + 1))
                        b.did(V.scalar_tensor_tensor(vy[:, w], ps[:, BP + AXS, w], ev_e[:, o, 4 + q:5 + q], vc[:, w], ALU.add, ALU.add))
                    b.settle()
                    V.scalar_tensor_tensor(split_in(x1[:, bass.ds(s, 1), :].rearrange("p a w -> p (a w)")), halves(vs), v1(0), halves(vy),
                                           ALU.add, ALU.add, accum_out=red[:, k:k + 1]).then_inc(y_done, 1)
                    dve.wait_ge(y_done, t + 1)
                    b.did(V.tensor_copy(cols[:, 0, bass.ds(s, 1)], red[:, k:k + 1]))

                u0 = i * (STRIPS // UNROLL)
                b = Steps(dve, b_steps, i * (STRIPS * DVE_B))
                build(b, 0, u0 + 1, t0)
                row_sums(b, 0, t0)
                assert b.n == 7
                with dve.Fori(0, STRIPS // UNROLL - 1) as j:
                    for k in range(UNROLL):
                        s = j * UNROLL + k
                        b = Steps(dve, b_steps, (t0 + s) * DVE_B + 7)
                        build(b, (k + 1) % UNROLL, u0 + j + 1 + (k + 1) // UNROLL, t0 + s + 1)
                        combine(b, k, s, t0 + s)
                        row_sums(b, (k + 1) % UNROLL, t0 + s + 1)
                        assert b.n == DVE_B, b.n
                for s in range(STRIPS - UNROLL, STRIPS):
                    b = Steps(dve, b_steps, (t0 + s) * DVE_B + 7)
                    if s + 1 < STRIPS:
                        build(b, (s + 1) % UNROLL, u0 + s // UNROLL + 1, t0 + s + 1)
                    combine(b, s % UNROLL, s, t0 + s)
                    if s + 1 < STRIPS:
                        row_sums(b, (s + 1) % UNROLL, t0 + s + 1)
                assert b.n == DVE_B - 7

                dve.wait_ge(y_done, t0 + STRIPS)
                dve.wait_ge(y_squared, t0 + STRIPS)
                b.settle()
                c.did(V.tensor_reduce(v1(ST1), cols[:, 0, 0:STRIPS], AX_X, ALU.add))
                V.tensor_reduce(v1(ST1 + 1), cols[:, 1, 0:STRIPS], AX_X, ALU.add).then_inc(v_sums1, 1)
                dve.wait_ge(p_stat1, i + 1)
                moments(c, 2, ps[:, BM, 0:2], 0)
                c.then(V.tensor_scalar(v1(MEANP), ps[:, BM, 2:3], float(-N), None, ALU.mult))
                V.tensor_scalar(colv, ps[:, BT, :], v1(MEANP), None, ALU.add).then_inc(v_colv, 1)
                dve.wait_ge(v_colv, i + 1)
                c.did(V.tensor_reduce(v1(SV), colv, AX_X, ALU.add))
                with dve.Fori(0, STRIPS) as s:
                    dve.wait_ge(dotted, (t0 + s) * 2)
                    V.scalar_tensor_tensor(vc, x1[:, bass.ds(s, 1), :].rearrange("p a w -> p (a w)"), 1.0, colv,
                                           ALU.mult, ALU.mult, accum_out=red[:, 0:1]).then_inc(dotted, 1)
                    dve.wait_ge(dotted, (t0 + s) * 2 + 1)
                    V.tensor_copy(cols[:, 2, bass.ds(s, 1)], red[:, 0:1]).then_inc(dotted, 1)
                dve.wait_ge(dotted, (t0 + STRIPS) * 2)
                c.settle()
                S, Q, D, GA, A_, B_, T1, T2 = (cols[:, k, 0:STRIPS] for k in range(8))
                c.then(V.tensor_tensor(v1(SV), v1(SV), v1(0), ALU.mult))
                c.then(V.tensor_scalar(GA, D, v1(SV), 0.0, ALU.subtract, ALU.is_gt))
                c.then(V.tensor_scalar(GA, GA, v1(1), None, ALU.mult))
                c.did(V.tensor_scalar(A_, GA, 1.0, None, ALU.add))
                c.then(V.tensor_scalar(B_, GA, v1(2), None, ALU.mult))
                c.did(V.tensor_tensor(T1, A_, S, ALU.mult))
                c.then(V.tensor_tensor(T2, A_, Q, ALU.mult))
                c.did(V.tensor_tensor(T2, T2, A_, ALU.mult))
                c.then(V.tensor_scalar(GA, B_, float(N), None, ALU.mult))
                c.then(V.scalar_tensor_tensor(D, T1, 2.0, GA, ALU.mult, ALU.add))
                c.did(V.tensor_tensor(D, D, B_, ALU.mult))
                c.then(V.tensor_tensor(T1, T1, GA, ALU.add))
                c.then(V.tensor_tensor(T2, T2, D, ALU.add))
                c.did(V.tensor_reduce(v1(ST), T1, AX_X, ALU.add))
                V.tensor_reduce(v1(ST + 1), T2, AX_X, ALU.add).then_inc(v_sums2, 1)
                dve.wait_ge(p_stat2, i + 1)
                c.then(V.tensor_copy(v1(MEANP), ps[:, BM, 0:1]))
                c.did(V.tensor_scalar(B_, B_, v1(MEANP), None, ALU.subtract))
                c.then(V.tensor_copy(v1(CM, 0, CO), ps[0:CO, BM, 2:3]))
                moments(c, 3, ps[:, BM, 4:6], ZV)

                def conv_weights(pad, loaded, done):
                    for k in range(UNROLL):
                        for e in (0, N + 1):
                            c.did(V.memset(cin[:, k, e:e + 1], 0.0) if pad is None else V.tensor_copy(cin[:, k, e:e + 1], pad))
                    dve.wait_ge(cw_loaded, loaded)
                    V.scalar_tensor_tensor(conv_s[:].rearrange("p a b c -> p (a b c)"), conv_w, v1(ZV + 1),
                                           conv_eye, ALU.mult, ALU.add).then_inc(done, 1)

                conv_weights(None, i * 48 + 32, v_conv2)
                with dve.Fori(0, STRIPS) as s:
                    xs = x1[:, bass.ds(s, 1), :].rearrange("p a w -> p (a w)")
                    V.tensor_scalar(xs, xs, cols[:, 4, bass.ds(s, 1)], cols[:, 5, bass.ds(s, 1)], ALU.mult, ALU.add).then_inc(gated, 1)
                for_sq = lambda v, slot, use, variant: conv_square(i, v, slot)

                def conv_square(i, v, slot):
                    n = i * CONV_STRIPS + v
                    dve.wait_ge(evicted, i * (2 * CONV_STRIPS) + v + 1 + CONV_CREDIT)
                    dve.wait_ge(c_squared, n + CONV_CREDIT)
                    dve.wait_ge(c_reduced, n)
                    V.scalar_tensor_tensor(vc[0:CO, :], cout[:, slot % 2, :], 1.0, cout[:, slot % 2, :], ALU.mult, ALU.mult,
                                           accum_out=red[0:CO, 0:1]).then_inc(c_squared, 1)
                    dve.wait_ge(c_squared, n + 1 + CONV_CREDIT)
                    V.tensor_copy(cols[0:CO, 3, bass.ds(v, 1)], red[0:CO, 0:1]).then_inc(c_reduced, 1)

                conv_strips(dve, for_sq)
                dve.wait_ge(c_reduced, (i + 1) * CONV_STRIPS)
                last = CONV_STRIPS - 1
                for q in (2, 3):
                    c.did(V.tensor_tensor(cols[0:CO, q, last:last + 1], cols[0:CO, q, last:last + 1], small[0:CO, 1:2], ALU.mult))
                c.settle()
                for q in (2, 3):
                    V.tensor_reduce(v1(ST + q - 2, 0, CO), cols[0:CO, q, 0:CONV_STRIPS], AX_X, ALU.add).then_inc(v_sums3, 1)
                dve.wait_ge(p_stat3, i + 1)
                moments(c, 4, ps[:, BM, 0:2], ZV)
                c.then(V.tensor_copy(v1(CM, 0, CO), ps[0:CO, BM, 2:3]))
                conv_weights(v1(ZV), i * 48 + 48, v_conv3)
                dve.wait_ge(p_bias3, i + 1)
                for var in range(3):
                    V.tensor_tensor(v1(BIAS3 + var, 0, CO), v1(CM, 0, CO), ps[0:CO, BM, 4 + var:5 + var], ALU.subtract).then_inc(v_bias3, 1)
                assert c.n == DVE_PREPS, c.n

        @block.tensor
        def _(pe):
            pe.sem_inc(a_projected, A_CREDIT)
            pe.sem_inc(mixed, MIXED_CREDIT)
            pe.sem_inc(convolved, CONV_CREDIT)
            pe.wait_ge(s_const, 13 * 16)
            pe.wait_ge(s_based, 1)

            def chunk(k):
                return lambda a: a.rearrange("p (h w q) -> p q h w", h=2, q=2)[:, k // 2, k % 2]

            def statistics(rng, sums, dst, tab, n):
                return pe.matmul(dst, tab[0:n, rng[0]:rng[1]], sums, start=True, stop=True)

            with pe.Fori(0, B) as i:
                def project(j, k, start, stop):
                    pe.wait_ge(a_loaded[k], (i * (STRIPS // UNROLL) + j + 1) * 48)
                    for q in range(4):
                        mm = pe.matmul(ps[:, 2 + q, 0:ZR], chunk(q)(xin[:, k, :]), tt[:, k, :], start=start, stop=stop)
                    mm.then_inc(a_projected, 1)

                pe.wait_ge(evicted, i * (2 * CONV_STRIPS) + CONV_CREDIT)
                for k in range(UNROLL):
                    project(0, k, k == 0, False)
                with pe.Fori(1, STRIPS // UNROLL - 1) as j:
                    for k in range(UNROLL):
                        project(j, k, False, False)
                for k in range(UNROLL):
                    project(STRIPS // UNROLL - 1, k, False, k == UNROLL - 1)

                pe.wait_ge(v_sums0, i + 1)
                statistics(G_OUT, vec[:, ST1:ST1 + 2], ps[:, BM, 0:2], gsel, P)
                statistics(G_Z, vec[:, ST1:ST1 + 2], ps[0:ZR, BM, 2:4], gsel, P).then_inc(p_stat, 1)
                pe.wait_ge(v_zt, i + 1)
                for k in range(4):
                    mm = pe.transpose(ps[0:ZR, BT, k * P:(k + 1) * P], zt[:, k, :], eye[:])
                mm.then_inc(p_zin, 1)
                for k in range(4):
                    mm = pe.matmul(ps[0:ZR, BH + (k < 2), 0:HW_], zt[:, k, :], hil[:, k, :], start=(k % 2 == 0), stop=(k % 2 == 1))
                mm.then_inc(p_zh, 1)
                pe.wait_ge(v_z, i + 1)
                for a in range(3):
                    pe.matmul(ps[0:48, BP + a, :], u_base[:, 2 * a, :] if a != AXC else u_base[:, 2, :], vc[0:ZR, :], start=True, stop=False)
                    pe.matmul(ps[0:48, BP + a, :], u_base[:, 2 * a + 1, :], vs[0:ZR, :], start=False, stop=True)
                for n, (k, g0) in enumerate(((0, 0), (1, 12), (2, 6), (3, 18))):
                    mm = pe.matmul(ps[0:48, BE, 0:6], u_base[:, k, :], gt[0:ZR, g0:g0 + 6], start=(n == 0), stop=(n == 3))
                mm.then_inc(p_u, 1)

                t0 = i * STRIPS
                u0 = i * (STRIPS // UNROLL)

                def turn(k, loads, t):
                    pe.wait_ge(x_loaded[k], loads * 48)
                    pe.wait_ge(xt_ready, t)
                    for q in range(4):
                        mm = pe.transpose(ps[:, BT, q * P:(q + 1) * P], chunk(q)(xin[:, k, :]), eye[:])
                    mm.then_inc(turned, 1)

                def hilbert(t):
                    pe.wait_ge(xt_ready, t + 1)
                    pe.wait_ge(h_ready, t * 2)
                    for q in range(4):
                        mm = pe.matmul(ps[:, BH + (q < 2), 0:HW_], xt[:, q, :], hil[:, q, :], start=(q % 2 == 0), stop=(q % 2 == 1))
                    mm.then_inc(h_done, 1)

                def mix(k, t):
                    o = k % 2
                    pe.wait_ge(w_ready, t + 1)
                    pe.wait_ge(g_ready, t + 1)
                    pe.wait_ge(y_done, t)
                    for g in range(2):
                        sl = slice(HP * g, HP * g + HP)
                        for a in range(2):
                            mm = pe.matmul(ps[sl, BE, 0:6], wst[:, o, g, a, :], gst[:, o, g, 6 * a:6 * a + 6], start=(a == 0), stop=(a == 1))
                    mm.then_inc(e_done, 1)
                    pe.wait_ge(h_ready, t * 2 + 2)
                    for a, done in ((AXB, pc_done), (AXC, ps_done)):
                        for g in range(2):
                            mm = pe.matmul(ps[HP * g:HP * g + HP, BP + a, :], wst[:, o, g, a, :], stack[:, o, g, :], start=True, stop=True)
                        mm.then_inc(done, 1)
                    for g in range(2):
                        pe.matmul(ps[HP * g:HP * g + HP, BP + AXS, :], strip[:, k, HP * g:HP * g + HP], u[:], start=True, stop=False)
                    for g in range(2):
                        mm = pe.matmul(ps[HP * g:HP * g + HP, BP + AXS, :], wst[:, o, g, AXS, :], stack[:, o, g, :], start=False, stop=True)
                    mm.then_inc(mixed, 1)

                pe.wait_ge(v_u, i * 2 + 2)
                turn(0, u0 + 1, t0)
                hilbert(t0)
                with pe.Fori(0, STRIPS // UNROLL - 1) as j:
                    for k in range(UNROLL):
                        s = j * UNROLL + k
                        turn((k + 1) % UNROLL, u0 + j + 1 + (k + 1) // UNROLL, t0 + s + 1)
                        mix(k, t0 + s)
                        hilbert(t0 + s + 1)
                for s in range(STRIPS - UNROLL, STRIPS):
                    if s + 1 < STRIPS:
                        turn((s + 1) % UNROLL, u0 + s // UNROLL + 1, t0 + s + 1)
                    mix(s % UNROLL, t0 + s)
                    if s + 1 < STRIPS:
                        hilbert(t0 + s + 1)

                pe.wait_ge(v_sums1, i + 1)
                pe.wait_ge(y_added, t0 + STRIPS)
                statistics(G_OUT, vec[:, ST1:ST1 + 2], ps[:, BM, 0:2], gsel, P)
                statistics(G_PART, vec[:, ST1:ST1 + 2], ps[:, BM, 2:4], gsel, P)
                pe.matmul(ps[:, BT, :], partner[:], acc, start=True, stop=True).then_inc(p_stat1, 1)
                pe.wait_ge(v_sums2, i + 1)
                statistics(G_OUT, vec[:, ST:ST + 2], ps[:, BM, 0:2], gsel, P)
                statistics(G_CO, vec[:, ST:ST + 2], ps[0:CO, BM, 2:4], gsel, P)
                statistics(G_CIN, vec[:, ST:ST + 2], ps[:, BM, 4:6], gsel, P).then_inc(p_stat2, 1)

                for ph in range(2):
                    if ph == 1:
                        pe.wait_ge(v_sums3, i * 2 + 2)
                        statistics((0, 128), vec[0:CO, ST:ST + 2], ps[:, BM, 0:2], csel, CO)
                        statistics((128, 128 + CO), vec[0:CO, ST:ST + 2], ps[0:CO, BM, 2:4], csel, CO).then_inc(p_stat3, 1)
                        pe.wait_ge(v_conv3, i + 1)
                        for var in range(3):
                            for kw in range(3):
                                mm = pe.matmul(ps[0:CO, BM, 4 + var:5 + var], conv_s[:, var, kw, :], vec[:, ZV:ZV + 1], start=(kw == 0), stop=(kw == 2))
                        mm.then_inc(p_bias3, 1)
                    else:
                        pe.wait_ge(v_conv2, i + 1)

                    def conv(v, slot, use, variant):
                        n = (i * 2 + ph) * CONV_STRIPS + v
                        pe.wait_ge(c_loaded[slot], (i * 2 + ph) * (16 * USES[slot]) + use * 16 + 16)
                        pe.wait_ge(evicted, n + 1 - UNROLL + CONV_CREDIT)
                        for kw in range(3):
                            mm = pe.matmul(ps[0:CO, 2 + slot, :], conv_s[:, variant, kw, :], cin[:, slot, kw:kw + N], start=(kw == 0), stop=(kw == 2))
                        mm.then_inc(convolved, 1)

                    conv_strips(pe, conv)


def kernel(x, L0_conv_w_real, L0_conv_w_imag, L0_conv_b_real, L0_conv_b_imag, L2_conv_W, L3_conv_weight):
    import numpy as _np
    import concourse.bacc as _bacc
    from concourse import mybir as _mybir
    from concourse.bass_utils import run_bass_kernel_spmd as _run

    a = [_np.asarray(v) for v in (L0_conv_w_real, L0_conv_w_imag, L0_conv_b_real, L0_conv_b_imag, L2_conv_W, L3_conv_weight)]
    arrays = {"x": _np.ascontiguousarray(x)}
    arrays.update(tables())
    arrays.update(placed(*a))
    nc = _bacc.Bacc("TRN2", target_bir_lowering=False, num_devices=1)
    args = {n: nc.dram_tensor(n, v.shape, _mybir.dt.from_np(v.dtype), kind="ExternalInput").ap() for n, v in arrays.items()}
    args["out"] = nc.dram_tensor("out", (B, C, N, N), _mybir.dt.float32, kind="ExternalOutput").ap()
    program(nc, **args)
    r = _run(nc, [arrays], core_ids=[0])
    return r.results[0]["out"]
```

```python
from contextlib import ExitStack

import numpy as np

import concourse.bass as bass
from concourse import mybir

F32 = mybir.dt.float32
ALU = mybir.AluOpType
ACT = mybir.ActivationFunctionType
AX_X = mybir.AxisListType.X

B, C, N = 8, 16, 512
P = 128
HP = P // 2
ROWS = 8
STRIPS = N // ROWS
UNROLL = 4
TILES = 4
TM = P // TILES
EPS = 1e-5
HALF = N // 2
NG = 24
HW_ = HALF + NG
AHEAD = 4 * UNROLL
COUTS = 4
SLOTS = 4
DOT_CREDIT = 2
FREE = 1
MIXED_CREDIT = STRIPS + UNROLL
CONV_CREDIT = 4
A_CREDIT = 4
AXB, AXC, AXS = 0, 1, 2
ZR = 96
UR = 80


def tables():
    n = np.arange(N)
    th = 2 * np.pi * n / N
    cos, sin = np.cos(th), np.sin(th)
    split = np.concatenate([n[::2], n[1::2]])
    t = n[None, :] - n[:, None]
    odd = t % 2 != 0
    hil = np.where(odd, (2.0 / N) / np.tan(np.where(odd, np.pi * t / N, 1.0)), 0.0)
    ev = (n % 2 == 0).astype(float)
    od = 1 - ev
    z = 0 * ev
    g_xc = [z, z, z, z, -ev * cos / N, -od * cos / N]
    g_hc = [z, z, 2 / N * od, 2 / N * ev, od * sin / N, ev * sin / N]
    g_xs = [z, z, z, z, -ev * sin / N, -od * sin / N]
    g_hs = [-2 / N * od, -2 / N * ev, z, z, -od * cos / N, -ev * cos / N]
    g = np.stack(g_xc + g_xs + g_hc + g_hs, 1)
    hil_t = np.zeros((P, 4, HW_))
    for k in range(4):
        rows = split[k * P:(k + 1) * P]
        cols = n[1::2] if k < 2 else n[::2]
        hil_t[:, k, :HALF] = hil[rows][:, cols]
        hil_t[:, k, HALF:] = g[rows]
    mean_fix = np.zeros((P, NG))
    mean_fix[:, 12 + 2:12 + 4] = -1.0
    mean_fix[:, 18:20] = 1.0
    trig_cols = np.broadcast_to(np.stack([cos[split], sin[split]]), (P, 2, N))

    p = np.arange(P)
    ch, r4, half = p % C, (p % HP) // C, p // HP
    strip = np.zeros((STRIPS, P, P + 4 + ZR))
    for s in range(STRIPS):
        row_out = ROWS * s + 4 * half + r4
        for k, f in enumerate((cos, sin, np.ones(N))):
            strip[s, C * k + ch, p] = f[row_out]
        strip[s, 64 + ch, p] = row_out == 0
        for gg in range(2):
            row = ROWS * s + 4 * gg + r4
            strip[s, :, P + 2 * gg] = cos[row]
            strip[s, :, P + 2 * gg + 1] = sin[row]
        row_in = ROWS * s + 4 * (1 - half) + r4
        for k, f in enumerate((np.ones(N), cos, sin)):
            strip[s, p, P + 4 + 32 * k + ch] = f[row_in] / N
    grp = ch // 2
    zc = np.arange(ZR) % 32
    dst = [grp, (p % 32) // 4, np.where(zc < C, zc // 2, -1), (grp + 4) % 8]
    scale = 1.0 / (2 * N * N)
    gsel = np.concatenate([(grp[:, None] == d[None, :]) * scale for d in dst], 1)
    partner = (ch[:, None] == (ch[None, :] + 8) % 16).astype(float)
    eye_mix = np.zeros((P, 2, 3, HP))
    for gg in range(2):
        for c in range(HP):
            eye_mix[HP * gg + c, gg, AXS, c] = 1.0
    eye_conv = np.zeros((P, 4, TM))
    for r in range(2):
        for c in range(C):
            eye_conv[32 * (r + 1) + 2 * c, 1, C * r + c] = 1.0
            eye_conv[32 * (r + 1) + 2 * c + 1, 2, C * r + c] = 1.0
    zsel = np.zeros((ZR, P + ZR))
    for k, d in enumerate((dst[0], dst[2])):
        zsel[:C, P * k:P * k + len(d)] = (np.arange(C)[:, None] // 2 == d[None, :]) / (2.0 * N)
    small = np.zeros((P, 1))
    small[:C, 0] = 1.0
    bias_rows = np.zeros((P, 2, N))
    bias_rows[64:64 + C, 0] = (split == 0)
    bias_rows[64:64 + C, 1] = -hil[0][split]
    f = lambda a: np.ascontiguousarray(a, dtype=np.float32)
    return {
        "t_eye": f(np.eye(P)), "t_hil": f(hil_t), "t_fix": f(mean_fix), "t_trig": f(trig_cols),
        "t_strip": f(strip), "t_gsel": f(gsel), "t_zsel": f(zsel), "t_partner": f(partner),
        "t_eye_mix": f(eye_mix), "t_eye_conv": f(eye_conv), "t_small": f(small), "t_bias": f(bias_rows),
    }


def placed(w_real, w_imag, b_real, b_imag, w2, w3):
    w = np.stack([w_real, w_imag])[:, :, :, ::-1, ::-1]
    w = w.transpose(1, 3, 4, 0, 2)
    mix = np.zeros((P, 3, 3, 2, HP), np.float32)
    uw = np.zeros((ZR, 3, 3, 2, C), np.float32)
    for c in range(C):
        for half in range(2):
            for r in range(4):
                mix[HP * half + C * r + c, :, :, :, C * r:C * r + C] = w[c]
        for k in range(3):
            uw[32 * k + c] = w[c]
    bias = np.zeros((P, 2), np.float32)
    bias[64:64 + C, 0] = b_real
    bias[64:64 + C, 1] = b_imag
    taps = (((1, 0),), ((0, 1), (1, 2)), ((0, 0), (1, 1)), ((0, 2),))
    convs = np.zeros((P, 2, 4, TM), np.float32)
    for l, wt in enumerate((w2, w3.reshape(C, C, 3, 3))):
        for m, pairs in enumerate(taps):
            for q, kw in pairs:
                for r in range(2):
                    for kh in range(3):
                        r0 = 32 * (r + kh) + q
                        convs[r0:r0 + 32:2, l, m, C * r:C * r + C] = wt[:, :, kh, kw].T
    return {"w_mix": mix, "w_u": uw, "w_bias": bias, "w_conv": convs}


class Steps:

    def __init__(self, eng, sem, base):
        self.eng, self.sem, self.base, self.n = eng, sem, base, 0

    def did(self, ins):
        ins.then_inc(self.sem, 1)
        self.n += 1

    def settle(self):
        self.eng.wait_ge(self.sem, self.base + self.n)

    def then(self, ins):
        self.did(ins)
        self.settle()


DVE_B = 15
MOMENTS = 5
DVE_PREPS = 93


def program(nc, x, t_eye, t_hil, t_fix, t_trig, t_strip, t_gsel, t_zsel, t_partner, t_eye_mix,
            t_eye_conv, t_small, t_bias, w_mix, w_u, w_bias, w_conv, out):
    with ExitStack() as ctx:
        def sb(name, *shape):
            return ctx.enter_context(nc.sbuf_tensor(name, list(shape), F32))

        def sem(name):
            return ctx.enter_context(nc.semaphore(name))

        in2 = nc.dram_tensor("in2", [N + 2, C, N], F32).ap()
        in3 = nc.dram_tensor("in3", [N + 2, C, N], F32).ap()

        ps = ctx.enter_context(nc.psum_tensor("ps", [P, 8, 512], F32))
        BT, BH, BP, BE, BZ = 0, 1, 3, 6, 7
        stat = ps[:, BE, 16:32]

        eye = sb("eye", P, P)
        hil = sb("hil", P, 4, HW_)
        fix = sb("fix", P, NG)
        trig = sb("trig", P, 2, N)
        gsel = sb("gsel", P, 128 + 128 + ZR + 128)
        zsel = sb("zsel", ZR, P + ZR)
        partner = sb("partner", P, P)
        small = sb("small", P, 1)
        bias_w = sb("bias_w", P, 2)
        mix_base = sb("mix_base", P, 3, 2, 3, HP)
        mix_s = sb("mix_s", P, 3, 2, 3, HP)
        eye_mix = sb("eye_mix", P, 2, 3, HP)
        u_base = sb("u_base", ZR, 6, 48)
        conv_w = sb("conv_w", P, 2, 4, TM)
        conv_eye = sb("conv_eye", P, 4, TM)
        conv_s = sb("conv_s", P, 4, TM)
        x1 = sb("x1", P, STRIPS, N)
        xin = sb("xin", P, UNROLL, N)
        cout = xin
        strip = sb("strip", P, UNROLL, P + 4 + ZR)
        shared = sb("shared", P, SLOTS * TILES * (HALF + 2))
        stack = shared[:, 0:4 * N].rearrange("p (b g w) -> p b g w", b=2, g=2)
        xa = shared[:, 4 * N:8 * N].rearrange("p (k w) -> p k w", k=UNROLL)
        cin = shared[:].rearrange("p (k t w) -> p k t w", k=SLOTS, t=TILES)
        xt = sb("xt", P, 4, P)
        wst = sb("wst", P, 2, 2, 3, HP)
        gp = sb("gp", P, 2, NG)
        gt = sb("gt", P, NG)
        gst = sb("gst", P, 2, 2, 12)
        ev_e = sb("ev_e", P, 2, 6)
        work = sb("work", P, 5, N)
        vc, vs, vy, junk, acc = (work[:, k, :] for k in range(5))
        colv = vs
        u = sb("u", P, N)
        zt = sb("zt", P, 4, ZR)
        cols = sb("cols", P, 8, STRIPS)
        vec = sb("vec", P, 32)
        red = sb("red", P, UNROLL)

        s_const = sem("constants_loaded")
        s_setup = sem("setup_steps")
        s_based = sem("setup_done")
        s_pool = sem("pool_zeroed")
        a_loaded = [sem(f"a_loaded{k}") for k in range(UNROLL)]
        a_table = [sem(f"a_table{k}") for k in range(UNROLL)]
        a_squared, a_projected = sem("a_squared"), sem("a_projected")
        v_xsq = sem("x_squares")
        d_prep, v_var, a_root = sem("dve_prep_steps"), sem("var_ready"), sem("root_ready")
        p_stat, p_zin, p_zh, p_u = sem("pe_stat"), sem("pe_zin"), sem("pe_zh"), sem("pe_u")
        v_sums0, v_zt, v_scaled, v_z, v_u = sem("sums0"), sem("zt_ready"), sem("mix_scaled"), sem("z_ready"), sem("u_ready")
        x_loaded = [sem(f"x_loaded{k}") for k in range(UNROLL)]
        turned, xt_ready, h_done, h_ready = sem("turned"), sem("xt_ready"), sem("h_done"), sem("h_ready")
        g_taken, g_ready, w_ready, e_done = sem("g_taken"), sem("g_ready"), sem("w_ready"), sem("e_done")
        pc_done, ps_done, mixed = sem("pc_done"), sem("ps_done"), sem("mixed")
        b_steps, y_done, y_squared, y_added = sem("b_steps"), sem("y_done"), sem("y_squared"), sem("y_added")
        acc_zero = sem("acc_zeroed")
        v_sums1, p_stat1, v_colv = sem("sums1"), sem("pe_stat1"), sem("colv_ready")
        dotted, dots_kept = sem("dotted"), sem("dots_kept")
        v_sums2, p_stat2, v_conv2 = sem("sums2"), sem("pe_stat2"), sem("conv2_weights")
        gated, v_gates = sem("gated"), sem("gates_ready")
        in2_stored = [sem(f"in2_stored{k}") for k in range(2)]
        c_loaded = [sem(f"c_loaded{k}") for k in range(SLOTS)]
        c_stored = [sem(f"c_stored{k}") for k in range(COUTS)]
        v_zero, pad2_stored = sem("zeroed"), sem("pad_rows2_stored")
        v_pad3, pad3_stored = sem("pad3_ready"), sem("pad_rows3_stored")
        convolved, evicted, c_squared, c_reduced = sem("convolved"), sem("evicted"), sem("c_squared"), sem("c_reduced")
        v_sums3, p_stat3, v_conv3, p_bias3, v_bias3 = sem("sums3"), sem("pe_stat3"), sem("conv3_weights"), sem("pe_bias3"), sem("bias3")

        block = ctx.enter_context(nc.Block())

        MEAN, RS, NEGM, VAR, MZ, MEANP, SV, BIAS3 = 0, 1, 2, 3, 5, 6, 7, 9
        ST, ST1, CM, XSQ, ZSUM, ZV = 12, 14, 16, 17, 18, 20

        def v1(k, p0=0, p1=P):
            return vec[p0:p1, k:k + 1]

        assert STRIPS % UNROLL == 0 and UNROLL % SLOTS == 0 and UNROLL % COUTS == 0

        G_OUT, G_CIN, G_Z, G_PART = (0, 128), (128, 256), (256, 256 + ZR), (256 + ZR, 384 + ZR)

        split_in = lambda a: a.rearrange("p (w q) -> p q w", q=2)
        halves = lambda a: a.rearrange("p (q w) -> p q w", q=2)

        @block.sync
        def _(sp):
            for dst, src in ((eye[:], t_eye), (hil[:], t_hil), (fix[:], t_fix), (trig[:], t_trig),
                             (gsel[:], t_gsel), (zsel[:], t_zsel), (conv_w[:], w_conv), (conv_eye[:], t_eye_conv), (partner[:], t_partner),
                             (small[:], t_small), (bias_w[:], w_bias), (eye_mix[:], t_eye_mix),
                             (x1[:, 0:3, :].rearrange("p a b -> p (a b)")[:, 0:1152], w_mix.rearrange("p a b c d -> p (a b c d)")),
                             (x1[0:ZR, 3:4, 0:288].rearrange("p a b -> p (a b)"), w_u.rearrange("p a b c d -> p (a b c d)")),
                             (x1[:, 4:6, :], t_bias)):
                sp.dma_start(dst, src).then_inc(s_const, 16)

            def load_x(i, s, slot, dst, loaded):
                for g in range(2):
                    src = x[i].rearrange("c (s g r) w -> s g r c w", g=2, r=4)[s, g]
                    sp.dma_start(dst[HP * (1 - g):HP * (2 - g), slot, :], src).then_inc(loaded[slot], 16)

            for k in range(COUTS):
                sp.sem_inc(c_stored[k], FREE)
            sp.wait_ge(v_zero, 1)
            for row in (0, N + 1):
                sp.dma_start(in2[row], acc[0:C, :]).then_inc(pad2_stored, 16)

            def load_next(image, s, t, k):
                sp.wait_ge(a_squared, t + 1)
                sp.wait_ge(a_projected, t + 1)
                load_x(image, s, k, xa, a_loaded)

            with sp.Fori(0, STRIPS // UNROLL) as j:
                for k in range(UNROLL):
                    s = j * UNROLL + k
                    load_next(0, s, s, k)
                    sp.dma_start(strip[:, k, :], t_strip[s]).then_inc(a_table[k], 16)

            def image(i, more):
                with sp.Fori(0, STRIPS // UNROLL) as j:
                    for k in range(UNROLL):
                        s = j * UNROLL + k
                        t = i * STRIPS + s
                        sp.wait_ge(c_stored[k], i * (2 * 16 // COUTS * STRIPS) + FREE)
                        sp.wait_ge(a_projected, t + STRIPS + 1 if more else B * STRIPS + A_CREDIT)
                        sp.wait_ge(mixed, t + 1 - UNROLL + MIXED_CREDIT)
                        load_x(i, s, k, xin, x_loaded)
                        sp.dma_start(strip[:, k, :], t_strip[s]).then_inc(x_loaded[k], 16)
                        if more:
                            sp.wait_ge(convolved, i * (2 * STRIPS) + CONV_CREDIT)
                            load_next(i + 1, s, t + STRIPS, k)
                G = STRIPS // UNROLL
                def store(g, e):
                    sp.wait_ge(gated, i * STRIPS + g * UNROLL + UNROLL)
                    dst = in2[1:N + 1].rearrange("(a s r) c w -> a (r c) s w", r=ROWS, s=UNROLL)
                    sp.dma_start(dst[g], x1[:, bass.ds(g * UNROLL, UNROLL), :]).then_inc(in2_stored[e], 16)

                def load(ph, s, k, stored=None):
                    slot = k % SLOTS
                    src = (in2, in3)[ph]
                    used = (i * 2 + ph) * STRIPS + s + 1 - SLOTS + CONV_CREDIT
                    views = [src[2 * h:2 * h + ((N - 2 * h + 2) // ROWS) * ROWS].rearrange(
                        "(s a r) c (q w) -> s (r c q) a w", a=2, r=4, q=2) for h in range(2)]
                    sp.wait_ge(pad2_stored if ph == 0 else pad3_stored, 32 if ph == 0 else (i + 1) * 32)
                    sp.wait_ge(v_conv2 if ph == 0 else v_conv3, i + 1)
                    sp.wait_ge(convolved, used)
                    if stored:
                        sp.wait_ge(*stored)
                    for h in range(2):
                        sp.dma_start(cin[:, slot].rearrange("p (a h) w -> p h a w", h=2)[:, h, :, 1:HALF + 1],
                                     views[h][s]).then_inc(c_loaded[slot], 16)

                def load_group(jj, e, store_next=True, last=False):
                    g = jj * 2 + e
                    h0 = i * (G // 2) + jj
                    known = (lambda v: v) if type(jj) is int else sp.snap
                    g2 = known(g + 2)
                    strips = [known(g * UNROLL + k) for k in range(UNROLL)]
                    for k in range(UNROLL):
                        stored = {0: (in2_stored[e], h0 * 16 + 16)}
                        if not last:
                            stored[UNROLL - 1] = (in2_stored[1 - e], (h0 + e) * 16 + 16)
                        load(0, strips[k], k, stored.get(k))
                        if k == 0 and store_next:
                            store(g2, e)

                store(0, 0)
                store(1, 1)
                with sp.Fori(0, G // 2 - 1) as jj:
                    for e in range(2):
                        load_group(jj, e)
                load_group(G // 2 - 1, 0, False)
                load_group(G // 2 - 1, 1, False, True)

                for k in range(COUTS):
                    sp.wait_ge(c_stored[k], (i * 2 + 1) * (16 // COUTS * STRIPS) + FREE)
                sp.wait_ge(v_pad3, i + 1)
                for row in (0, N + 1):
                    sp.dma_start(in3[row], vy[0:C, :]).then_inc(pad3_stored, 16)
                with sp.Fori(0, STRIPS // UNROLL) as j:
                    for k in range(UNROLL):
                        load(1, j * UNROLL + k, k)
            with sp.Fori(0, B - 1) as i:
                image(i, True)
            image(B - 1, False)
            for k in range(COUTS):
                sp.wait_ge(c_stored[k], B * 2 * (16 // COUTS) * STRIPS + FREE)

        @block.gpsimd
        def _(pool):
            pool.sem_inc(y_added, FREE)
            nc.gpsimd.memset(u[:], 0.0).then_inc(s_pool, 1)
            nc.gpsimd.memset(u_base[:], 0.0).then_inc(s_pool, 1)
            with pool.Fori(0, B) as i:
                with pool.Fori(0, STRIPS) as s:
                    t = i * STRIPS + s
                    pool.wait_ge(acc_zero, i + 1)
                    pool.wait_ge(y_done, t + 1 + FREE)
                    pool.wait_ge(y_added, t + FREE)
                    nc.gpsimd.tensor_tensor(acc, acc, x1[:, bass.ds(s, 1), :].rearrange("p a w -> p (a w)"), ALU.add).then_inc(y_added, 1)

        @block.scalar
        def _(act):
            act.sem_inc(a_squared, A_CREDIT)
            act.sem_inc(evicted, CONV_CREDIT)
            for signal in (y_squared, xt_ready, h_ready):
                act.sem_inc(signal, FREE)
            def square_next(s, t, loads, k):
                act.wait_ge(a_loaded[k], loads * 32)
                nc.scalar.activation(junk, xa[:, k, :], ACT.Square, accum_out=cols[:, 6, bass.ds(s, 1)]).then_inc(a_squared, 1)

            with act.Fori(0, STRIPS // UNROLL) as j:
                for k in range(UNROLL):
                    act.wait_ge(a_squared, j * UNROLL + k + A_CREDIT)
                    square_next(j * UNROLL + k, j * UNROLL + k, j + 1, k)

            def image(i, more):
                def root(n, dst, p1=P):
                    act.wait_ge(v_var, i * MOMENTS + n + 1)
                    nc.scalar.activation(v1(dst + 1, 0, p1), v1(dst + 3, 0, p1), ACT.Sqrt).then_inc(a_root, 1)

                root(0, 0)
                root(1, ZV, ZR)
                act.wait_ge(v_scaled, i + 1)

                def bring(t, loads, k):
                    act.wait_ge(x_loaded[k], loads * 48)
                    act.wait_ge(mixed, t - 1 + MIXED_CREDIT)
                    b = k % 2
                    nc.scalar.activation(halves(stack[0:HP, b, 0, :]), split_in(xin[HP:P, k, :]), ACT.Identity,
                                         bias=v1(NEGM, HP, P))
                    nc.scalar.activation(halves(stack[HP:P, b, 1, :]), split_in(xin[0:HP, k, :]), ACT.Identity,
                                         bias=v1(NEGM, 0, HP))
                    act.wait_ge(turned, t + 1)
                    act.wait_ge(h_done, t + FREE)
                    nc.scalar.activation(xt[:].rearrange("p a b -> p (a b)"), ps[:, BT, :], ACT.Identity).then_inc(xt_ready, 1)
                    act.wait_ge(h_done, t + 1 + FREE)
                    act.wait_ge(g_ready, t + FREE)
                    nc.scalar.activation(gp[:], ps[:, BH:BH + 2, HALF:HW_], ACT.Identity).then_inc(g_taken, 1)
                    nc.scalar.activation(halves(stack[HP:P, b, 0, :]), ps[HP:P, BH:BH + 2, 0:HALF], ACT.Identity).then_inc(h_ready, 1)
                    nc.scalar.activation(halves(stack[0:HP, b, 1, :]), ps[0:HP, BH:BH + 2, 0:HALF], ACT.Identity).then_inc(h_ready, 1)

                def min_squared(t):
                    return t + STRIPS + A_CREDIT if more else B * STRIPS + A_CREDIT

                def square(t, s):
                    act.wait_ge(y_done, t + 1 + FREE)
                    act.wait_ge(y_squared, t + FREE)
                    act.wait_ge(a_squared, min_squared(t))
                    nc.scalar.activation(junk, x1[:, bass.ds(s, 1), :].rearrange("p a w -> p (a w)"), ACT.Square,
                                         accum_out=cols[:, 1, bass.ds(s, 1)]).then_inc(y_squared, 1)

                u0 = i * (STRIPS // UNROLL)
                t0 = i * STRIPS
                bring(t0, u0 + 1, 0)
                with act.Fori(0, STRIPS // UNROLL - 1) as j:
                    for k in range(UNROLL):
                        s = j * UNROLL + k
                        bring(t0 + s + 1, u0 + j + 1 + (k + 1) // UNROLL, (k + 1) % UNROLL)
                        square(t0 + s, s)
                        if more:
                            act.wait_ge(y_squared, t0 + s + 1 + FREE)
                            square_next(s, t0 + STRIPS + s, u0 + STRIPS // UNROLL + j + 1, k)
                for s in range(STRIPS - UNROLL, STRIPS):
                    if s + 1 < STRIPS:
                        bring(t0 + s + 1, u0 + s // UNROLL + 1, (s + 1) % UNROLL)
                    square(t0 + s, s)
                    if more:
                        act.wait_ge(y_squared, t0 + s + 1 + FREE)
                        square_next(s, t0 + STRIPS + s, u0 + STRIPS // UNROLL + s // UNROLL + 1, s % UNROLL)

                root(2, 0)
                root(3, ZV)
                for ph in range(2):
                    if ph == 1:
                        root(4, ZV)
                    act.wait_ge(v_gates if ph == 0 else v_bias3, i + 1)
                    if ph == 0:
                        def gate(s):
                            xs = x1[:, bass.ds(s, 1), :].rearrange("p a w -> p (a w)")
                            nc.scalar.activation(xs, xs, ACT.Identity, scale=cols[:, 4, bass.ds(s, 1)],
                                                 bias=cols[:, 5, bass.ds(s, 1)]).then_inc(gated, 1)
                        for k in range(AHEAD):
                            gate(k)

                    def evict(j, more):
                        for k in range(UNROLL):
                            s = j * UNROLL + k
                            n = (i * 2 + ph) * STRIPS + s
                            if more:
                                gate(s + AHEAD)
                            o = k % COUTS
                            act.wait_ge(convolved, n + 1 + CONV_CREDIT)
                            act.wait_ge(c_stored[o], (n - k) * (16 // COUTS) + FREE)
                            if ph == 0:
                                act.wait_ge(c_squared, i * STRIPS + s + 1 - COUTS + CONV_CREDIT)
                                nc.scalar.activation(cout[:, o, :], ps[:, 2 + k % 4, :], ACT.Identity, bias=v1(MEANP),
                                                     accum_out=cols[:, 2, bass.ds(s, 1)]).then_inc(evicted, 1)
                            else:
                                nc.scalar.activation(cout[:, o, :].rearrange("p (w q) -> p q w", q=2), halves(ps[:, 2 + k % 4, :]),
                                                     ACT.Identity, bias=v1(BIAS3)).then_inc(evicted, 1)
                            act.wait_ge(evicted, n + 1 + CONV_CREDIT)
                            dst = (in3[1:N + 1].rearrange("(s r) c w -> s (r c) w", r=ROWS) if ph == 0
                                   else out[i].rearrange("c (s r) w -> s r c w", r=ROWS))
                            act.dma_start(dst[s], cout[:, o, :]).then_inc(c_stored[o], 16)

                    ahead = AHEAD // UNROLL if ph == 0 else 0
                    with act.Fori(0, STRIPS // UNROLL - ahead) as j:
                        evict(j, ph == 0)
                    for j in range(STRIPS // UNROLL - ahead, STRIPS // UNROLL):
                        evict(j, False)

            with act.Fori(0, B - 1) as i:
                image(i, True)
            image(B - 1, False)

        @block.vector
        def _(dve):
            V = nc.vector
            dve.sem_inc(c_squared, CONV_CREDIT)
            dve.sem_inc(dotted, DOT_CREDIT)
            for signal in (g_ready, y_done, dots_kept, c_reduced):
                dve.sem_inc(signal, FREE)
            st = Steps(dve, s_setup, 0)
            dve.wait_ge(s_const, 15 * 16)
            dve.wait_ge(s_pool, 2)
            wm = x1[:, 0:3, :].rearrange("p a b -> p (a b)")[:, 0:1152].rearrange("p (a b c d) -> p a b c d", a=3, b=3, c=2)
            wu = x1[0:ZR, 3:4, 0:288].rearrange("p a b -> p (a b)").rearrange("p (a b c d) -> p a b c d", a=3, b=3, c=2)
            tmp = x1[:, 8:16, :].rearrange("p a b -> p (a b)")
            q3 = tmp[:, 0:1152].rearrange("p (j b c d) -> p j b c d", j=3, b=3, c=2)
            pm = tmp[:, 1152:1152 + 768].rearrange("p (j f c d) -> p j f c d", j=3, f=2, c=2)
            fl = lambda a: a.rearrange("p b c d -> p (b c d)")
            st.did(V.tensor_copy(fl(q3[:, 0]), fl(wm[:, 1])))
            st.did(V.tensor_tensor(fl(q3[:, 1]), fl(wm[:, 2]), fl(wm[:, 0]), ALU.add))
            st.then(V.tensor_tensor(fl(q3[:, 2]), fl(wm[:, 2]), fl(wm[:, 0]), ALU.subtract))
            for j in range(3):
                for f, op in enumerate((ALU.add, ALU.subtract)):
                    st.did(V.tensor_tensor(pm[:, j, f], q3[:, j, 2], q3[:, j, 0], op))
            st.settle()
            for j in range(3):
                re, im = ((1, 0), (1, 1)) if j < 2 else ((1, 1), (-1, 0))
                for g in range(2):
                    for kind in range(2):
                        h0 = HP * (g ^ kind)
                        sl = slice(h0, h0 + HP)
                        for a in range(3):
                            which, sgn = ((re, 1), (im, -1)) [kind] if a != AXC else ((im, 1), (re, 1))[kind]
                            src = q3[sl, j, 1, which[1]] if a == AXS else pm[sl, j, a, which[1]]
                            st.did(V.tensor_scalar(mix_base[sl, j, g, a, :], src, float(which[0] * sgn), None, ALU.mult))
            pu = tmp[0:ZR, 2048:2048 + 192].rearrange("p (k f c d) -> p k f c d", k=3, f=2, c=2)
            for d1 in (0, 2):
                for f, op in enumerate((ALU.add, ALU.subtract)):
                    st.did(V.tensor_tensor(pu[:, d1, f], wu[:, d1, 2], wu[:, d1, 0], op))
            st.settle()
            for z, blk, d1, re, im in ((0, 0, 2, (1, 0), (1, 1)), (0, 1, 2, (1, 1), (-1, 0)),
                                       (1, 2, 0, (1, 0), (1, 1)), (2, 2, 0, (-1, 1), (1, 0))):
                sl = slice(32 * z, 32 * z + C)
                for k, (which, sgn, f) in enumerate(((re, 1, 0), (im, -1, 0), (im, 1, 1), (re, 1, 1), (re, 1, 2), (im, -1, 2))):
                    src = wu[sl, d1, 1, which[1]] if f == 2 else pu[sl, d1, f, which[1]]
                    st.did(V.tensor_scalar(u_base[sl, k, 16 * blk:16 * blk + 16], src, float(-which[0] * sgn), None, ALU.mult))
            sl = slice(64, 64 + C)
            br = x1[:, 4:6, :]
            st.then(V.tensor_scalar(u[sl, :], br[sl, 0, :], bias_w[sl, 0:1], None, ALU.mult))
            V.scalar_tensor_tensor(u[sl, :], br[sl, 1, :], bias_w[sl, 1:2], u[sl, :], ALU.mult, ALU.add).then_inc(s_based, 1)
            dve.wait_ge(s_based, 1)

            def moments(i, c, n, src, dst, p1=P):
                mean, rs, neg, var, t = (v1(dst + k, 0, p1) for k in (0, 1, 2, 3, 4))
                c.then(V.tensor_copy(vec[0:p1, dst:dst + 2], src))
                c.did(V.tensor_scalar(neg, mean, -1.0, None, ALU.mult))
                c.then(V.tensor_tensor(var, mean, mean, ALU.mult))
                c.then(V.tensor_tensor(var, rs, var, ALU.subtract))
                V.tensor_scalar(var, var, 0.0, EPS, ALU.max, ALU.add).then_inc(v_var, 1)
                dve.wait_ge(a_root, i * MOMENTS + n + 1)
                c.then(V.reciprocal(rs, rs))
                c.then(V.tensor_tensor(t, rs, rs, ALU.mult))
                c.then(V.tensor_tensor(t, t, var, ALU.mult))
                c.then(V.tensor_scalar(t, t, -0.5, 1.5, ALU.mult, ALU.add))
                c.then(V.tensor_tensor(rs, rs, t, ALU.mult))

            V.memset(acc, 0.0).then_inc(v_zero, 1)

            def take_next(n):
                dve.wait_ge(a_squared, n * STRIPS + STRIPS + A_CREDIT)
                V.tensor_reduce(v1(XSQ), cols[:, 6, :], AX_X, ALU.add).then_inc(v_xsq, 1)
                dve.wait_ge(a_projected, n * STRIPS + STRIPS + A_CREDIT)
                V.tensor_copy(zt[:].rearrange("p a b -> p (a b)"), ps[:, BZ, 0:4 * ZR]).then_inc(v_zt, 1)

            take_next(0)

            def image(i, more):
                c = Steps(dve, d_prep, i * DVE_PREPS)
                dve.wait_ge(pad2_stored, 32)
                V.memset(acc, 0.0).then_inc(acc_zero, 1)
                dve.wait_ge(p_zin, i + 1)
                V.tensor_reduce(v1(ZSUM, 0, ZR), ps[0:ZR, BT, :], AX_X, ALU.add).then_inc(v_sums0, 1)
                dve.wait_ge(p_stat, i + 1)
                moments(i, c, 0, stat[:, 0:2], 0)
                moments(i, c, 1, stat[0:ZR, 2:4], ZV, ZR)
                c.then(V.tensor_tensor(v1(MZ, 0, ZR), v1(ZV, 0, ZR), small[0:ZR, 0:1], ALU.mult))
                flat = lambda a: a.rearrange("p g a o -> p (g a o)")
                for jj in (1, 2):
                    c.did(V.tensor_scalar(flat(mix_s[:, jj]), flat(mix_base[:, jj]), v1(1), None, ALU.mult))
                V.scalar_tensor_tensor(flat(mix_s[:, 0]), flat(mix_base[:, 0]), v1(1), flat(eye_mix[:]), ALU.mult, ALU.add).then_inc(v_scaled, 1)
                dve.wait_ge(v_scaled, i + 1)
                zs, zhs, zg = vc, vs, gt
                dve.wait_ge(p_zin, i + 1)
                c.did(V.tensor_scalar(zs[0:ZR, :], ps[0:ZR, BT, :], v1(MZ, 0, ZR), v1(ZV + 1, 0, ZR), ALU.subtract, ALU.mult))
                dve.wait_ge(p_zh, i + 1)
                c.did(V.tensor_scalar(halves(zhs[0:ZR, :]), ps[0:ZR, BH:BH + 2, 0:HALF], v1(ZV + 1, 0, ZR), None, ALU.mult))
                c.then(V.scalar_tensor_tensor(zg[0:ZR, :], fix[0:ZR, :], v1(MZ, 0, ZR), ps[0:ZR, BH, HALF:HW_], ALU.mult, ALU.add))
                c.then(V.tensor_tensor(zg[0:ZR, :], zg[0:ZR, :], ps[0:ZR, BH + 1, HALF:HW_], ALU.add))
                V.tensor_scalar(zg[0:ZR, :], zg[0:ZR, :], v1(ZV + 1, 0, ZR), None, ALU.mult).then_inc(v_z, 1)
                dve.wait_ge(p_u, i + 1)
                c.then(V.tensor_copy(ev_e[0:48, 0, :], ps[0:48, BE, 0:6]))
                for q in range(2):
                    w = slice(HALF * q, HALF * (q + 1))
                    c.did(V.scalar_tensor_tensor(vy[0:48, w], ps[0:48, BP + AXB, w], ev_e[0:48, 0, q:q + 1], trig[0:48, 0, w], ALU.add, ALU.mult))
                    c.did(V.scalar_tensor_tensor(u[0:48, w], ps[0:48, BP + AXC, w], ev_e[0:48, 0, 2 + q:3 + q], trig[0:48, 1, w], ALU.add, ALU.mult))
                c.settle()
                c.then(V.tensor_tensor(vy[0:48, :], vy[0:48, :], u[0:48, :], ALU.add))
                for q in range(2):
                    w = slice(HALF * q, HALF * (q + 1))
                    V.scalar_tensor_tensor(u[0:48, w], ps[0:48, BP + AXS, w], ev_e[0:48, 0, 4 + q:5 + q], vy[0:48, w], ALU.add, ALU.add).then_inc(v_u, 1)
                dve.wait_ge(v_u, i * 2 + 2)

                t0 = i * STRIPS

                def build(b, k, loads, t):
                    dve.wait_ge(x_loaded[k], loads * 48)
                    dve.wait_ge(mixed, t - 1 + MIXED_CREDIT)
                    fg = lambda a: a.rearrange("p a o -> p (a o)")
                    for g in range(2):
                        b.did(V.scalar_tensor_tensor(fg(wst[:, k % 2, g]), fg(mix_s[:, 1, g]), strip[:, k, P + 2 * g:P + 2 * g + 1], fg(mix_s[:, 0, g]), ALU.mult, ALU.add))
                    b.settle()
                    b.did(V.scalar_tensor_tensor(fg(wst[:, k % 2, 0]), fg(mix_s[:, 2, 0]), strip[:, k, P + 1:P + 2], fg(wst[:, k % 2, 0]), ALU.mult, ALU.add))
                    V.scalar_tensor_tensor(fg(wst[:, k % 2, 1]), fg(mix_s[:, 2, 1]), strip[:, k, P + 3:P + 4], fg(wst[:, k % 2, 1]), ALU.mult, ALU.add).then_inc(w_ready, 1)

                def row_sums(b, k, t):
                    dve.wait_ge(g_taken, t + 1)
                    dve.wait_ge(g_ready, t + FREE)
                    b.then(V.scalar_tensor_tensor(gt[:], fix[:], v1(0), gp[:, 0, :], ALU.mult, ALU.add))
                    o = k % 2
                    gx, gh = slice(0, 12), slice(12, 24)
                    b.did(V.tensor_tensor(gst[0:HP, o, 0, :], gt[HP:P, gx], gp[HP:P, 1, gx], ALU.add))
                    b.did(V.tensor_tensor(gst[HP:P, o, 0, :], gt[HP:P, gh], gp[HP:P, 1, gh], ALU.add))
                    b.did(V.tensor_tensor(gst[0:HP, o, 1, :], gt[0:HP, gh], gp[0:HP, 1, gh], ALU.add))
                    V.tensor_tensor(gst[HP:P, o, 1, :], gt[0:HP, gx], gp[0:HP, 1, gx], ALU.add).then_inc(g_ready, 1)

                def combine(b, k, s, t):
                    o = k % 2
                    dve.wait_ge(e_done, t + 1)
                    b.then(V.tensor_copy(ev_e[:, o, :], ps[:, BE, 0:6]))
                    dve.wait_ge(y_done, t + FREE)
                    for a, done, dst in ((AXB, pc_done, vc), (AXC, ps_done, vs)):
                        dve.wait_ge(done, t + 1)
                        for q in range(2):
                            w = slice(HALF * q, HALF * (q + 1))
                            b.did(V.scalar_tensor_tensor(dst[:, w], ps[:, BP + a, w], ev_e[:, o, 2 * a + q:2 * a + q + 1], trig[:, a, w], ALU.add, ALU.mult))
                    b.settle()
                    dve.wait_ge(mixed, t + 1 + MIXED_CREDIT)
                    for q in range(2):
                        w = slice(HALF * q, HALF * (q + 1))
                        b.did(V.scalar_tensor_tensor(vy[:, w], ps[:, BP + AXS, w], ev_e[:, o, 4 + q:5 + q], vc[:, w], ALU.add, ALU.add))
                    b.settle()
                    V.scalar_tensor_tensor(x1[:, bass.ds(s, 1), :].rearrange("p a w -> p (a w)"), vs, v1(0), vy,
                                           ALU.add, ALU.add, accum_out=red[:, k:k + 1]).then_inc(y_done, 1)
                    dve.wait_ge(y_done, t + 1 + FREE)
                    b.did(V.tensor_copy(cols[:, 0, bass.ds(s, 1)], red[:, k:k + 1]))

                u0 = i * (STRIPS // UNROLL)
                b = Steps(dve, b_steps, i * (STRIPS * DVE_B))
                build(b, 0, u0 + 1, t0)
                row_sums(b, 0, t0)
                assert b.n == 7
                with dve.Fori(0, STRIPS // UNROLL - 1) as j:
                    for k in range(UNROLL):
                        s = j * UNROLL + k
                        b = Steps(dve, b_steps, (t0 + s) * DVE_B + 7)
                        build(b, (k + 1) % UNROLL, u0 + j + 1 + (k + 1) // UNROLL, t0 + s + 1)
                        combine(b, k, s, t0 + s)
                        row_sums(b, (k + 1) % UNROLL, t0 + s + 1)
                        assert b.n == DVE_B, b.n
                for s in range(STRIPS - UNROLL, STRIPS):
                    b = Steps(dve, b_steps, (t0 + s) * DVE_B + 7)
                    if s + 1 < STRIPS:
                        build(b, (s + 1) % UNROLL, u0 + s // UNROLL + 1, t0 + s + 1)
                    combine(b, s % UNROLL, s, t0 + s)
                    if s + 1 < STRIPS:
                        row_sums(b, (s + 1) % UNROLL, t0 + s + 1)
                assert b.n == DVE_B - 7

                if more:
                    take_next(i + 1)
                dve.wait_ge(y_done, t0 + STRIPS + FREE)
                dve.wait_ge(y_squared, t0 + STRIPS + FREE)
                b.settle()
                c.did(V.tensor_reduce(v1(ST1), cols[:, 0, 0:STRIPS], AX_X, ALU.add))
                V.tensor_reduce(v1(ST1 + 1), cols[:, 1, 0:STRIPS], AX_X, ALU.add).then_inc(v_sums1, 1)
                dve.wait_ge(p_stat1, i + 1)
                moments(i, c, 2, stat[:, 0:2], 0)
                c.then(V.tensor_scalar(v1(MEANP), stat[:, 2:3], float(-N), None, ALU.mult))
                V.tensor_scalar(colv, ps[:, BT, :], v1(MEANP), None, ALU.add).then_inc(v_colv, 1)
                dve.wait_ge(v_colv, i + 1)
                c.did(V.tensor_reduce(v1(SV), colv, AX_X, ALU.add))
                with dve.Fori(0, STRIPS // UNROLL) as j:
                    g0 = u0 + j
                    dve.wait_ge(dots_kept, g0 + FREE)
                    for k in range(UNROLL):
                        dve.wait_ge(dotted, g0 * UNROLL + k - 1 + DOT_CREDIT)
                        V.scalar_tensor_tensor((vc, vy)[k % 2], x1[:, bass.ds(j * UNROLL + k, 1), :].rearrange("p a w -> p (a w)"), 1.0, colv,
                                               ALU.mult, ALU.mult, accum_out=red[:, k:k + 1]).then_inc(dotted, 1)
                    dve.wait_ge(dotted, g0 * UNROLL + UNROLL + DOT_CREDIT)
                    V.tensor_copy(cols[:, 2, bass.ds(j * UNROLL, UNROLL)], red[:]).then_inc(dots_kept, 1)
                dve.wait_ge(dots_kept, u0 + STRIPS // UNROLL + FREE)
                c.settle()
                S, Q, D, GA, A_, B_, T1, T2 = (cols[:, k, 0:STRIPS] for k in range(8))
                c.then(V.tensor_tensor(v1(SV), v1(SV), v1(0), ALU.mult))
                c.then(V.tensor_scalar(GA, D, v1(SV), 0.0, ALU.subtract, ALU.is_gt))
                c.then(V.tensor_scalar(GA, GA, v1(1), None, ALU.mult))
                c.did(V.tensor_scalar(A_, GA, 1.0, None, ALU.add))
                c.then(V.tensor_scalar(B_, GA, v1(2), None, ALU.mult))
                c.did(V.tensor_tensor(T1, A_, S, ALU.mult))
                c.then(V.tensor_tensor(T2, A_, Q, ALU.mult))
                c.did(V.tensor_tensor(T2, T2, A_, ALU.mult))
                c.then(V.tensor_scalar(GA, B_, float(N), None, ALU.mult))
                c.then(V.scalar_tensor_tensor(D, T1, 2.0, GA, ALU.mult, ALU.add))
                c.did(V.tensor_tensor(D, D, B_, ALU.mult))
                c.then(V.tensor_tensor(T1, T1, GA, ALU.add))
                c.then(V.tensor_tensor(T2, T2, D, ALU.add))
                c.did(V.tensor_reduce(v1(ST), T1, AX_X, ALU.add))
                V.tensor_reduce(v1(ST + 1), T2, AX_X, ALU.add).then_inc(v_sums2, 1)
                dve.wait_ge(p_stat2, i + 1)
                c.then(V.tensor_copy(v1(MEANP), stat[:, 0:1]))
                V.tensor_scalar(B_, B_, v1(MEANP), None, ALU.subtract).then_inc(v_gates, 1)
                moments(i, c, 3, stat[:, 4:6], ZV)

                def conv_weights(pad, layer, done):
                    for k in range(SLOTS):
                        for e in (0, HALF + 1):
                            c.did(V.memset(cin[:, k, :, e:e + 1], 0.0) if pad is None
                                  else V.tensor_scalar(cin[:, k, :, e:e + 1], trig[:, 0, 0:TILES], 0.0, pad, ALU.mult, ALU.add))
                    flat_c = lambda a: a.rearrange("p m o -> p (m o)")
                    V.scalar_tensor_tensor(flat_c(conv_s[:]), flat_c(conv_w[:, layer]), v1(ZV + 1),
                                           flat_c(conv_eye[:]), ALU.mult, ALU.add).then_inc(done, 1)

                conv_weights(None, 0, v_conv2)
                with dve.Fori(0, STRIPS // UNROLL) as j:
                    dve.wait_ge(c_reduced, u0 + j + FREE)
                    for k in range(UNROLL):
                        s = j * UNROLL + k
                        n = i * STRIPS + s
                        dve.wait_ge(evicted, i * (2 * STRIPS) + s + 1 + CONV_CREDIT)
                        dve.wait_ge(c_squared, n + CONV_CREDIT - 1)
                        V.scalar_tensor_tensor((vc, vs)[k % 2], cout[:, k % COUTS, :], 1.0, cout[:, k % COUTS, :], ALU.mult, ALU.mult,
                                               accum_out=red[:, k:k + 1]).then_inc(c_squared, 1)
                    dve.wait_ge(c_squared, i * STRIPS + j * UNROLL + UNROLL + CONV_CREDIT)
                    V.tensor_copy(cols[:, 3, bass.ds(j * UNROLL, UNROLL)], red[:]).then_inc(c_reduced, 1)
                dve.wait_ge(c_reduced, u0 + STRIPS // UNROLL + FREE)
                for q in (2, 3):
                    V.tensor_reduce(v1(ST + q - 2), cols[:, q, :], AX_X, ALU.add).then_inc(v_sums3, 1)
                dve.wait_ge(p_stat3, i + 1)
                c.then(V.tensor_copy(v1(CM), stat[:, 2:3]))
                V.tensor_scalar(vy[0:C, :], trig[0:C, 0, :], 0.0, v1(CM, 0, C), ALU.mult, ALU.add).then_inc(v_pad3, 1)
                moments(i, c, 4, stat[:, 0:2], ZV)
                conv_weights(v1(ZV), 1, v_conv3)
                dve.wait_ge(p_bias3, i + 1)
                V.tensor_tensor(v1(BIAS3), v1(CM), stat[:, 4:5], ALU.subtract).then_inc(v_bias3, 1)
                assert c.n == DVE_PREPS, c.n

            with dve.Fori(0, B - 1) as i:
                image(i, True)
            image(B - 1, False)

        @block.tensor
        def _(pe):
            pe.sem_inc(a_projected, A_CREDIT)
            pe.sem_inc(mixed, MIXED_CREDIT)
            pe.sem_inc(convolved, CONV_CREDIT)
            pe.sem_inc(h_done, FREE)
            pe.wait_ge(s_const, 15 * 16)
            pe.wait_ge(s_based, 1)

            def chunk(k):
                return lambda a: a.rearrange("p (h w q) -> p q h w", h=2, q=2)[:, k // 2, k % 2]

            def statistics(rng, sums, dst, tab, n):
                return pe.matmul(dst, tab[0:n, rng[0]:rng[1]], sums, start=True, stop=True)

            def project(k, first):
                for q in range(4):
                    mm = pe.matmul(ps[:, BZ, ZR * q:ZR * (q + 1)], chunk(q)(xa[:, k, :]), strip[:, k, P + 4:P + 4 + ZR],
                                   start=first and q == 0, stop=False, skip_group_check=True)
                mm.then_inc(a_projected, 1)

            for k in range(UNROLL):
                pe.wait_ge(a_loaded[k], 32)
                pe.wait_ge(a_table[k], 16)
                project(k, k == 0)
            with pe.Fori(1, STRIPS // UNROLL) as j:
                for k in range(UNROLL):
                    pe.wait_ge(a_loaded[k], j * 32 + 32)
                    pe.wait_ge(a_table[k], j * 16 + 16)
                    project(k, False)

            def image(i, more):
                pe.wait_ge(v_zt, i + 1)
                pe.wait_ge(evicted, i * (2 * STRIPS) + CONV_CREDIT)
                for k in range(4):
                    mm = pe.transpose(ps[0:ZR, BT, k * P:(k + 1) * P], zt[:, k, :], eye[:])
                mm.then_inc(p_zin, 1)
                for k in range(4):
                    mm = pe.matmul(ps[0:ZR, BH + (k < 2), 0:HW_], zt[:, k, :], hil[:, k, :], start=(k % 2 == 0), stop=(k % 2 == 1))
                mm.then_inc(p_zh, 1)
                pe.wait_ge(v_sums0, i + 1)
                pe.wait_ge(v_xsq, i + 1)
                pe.matmul(stat[:, 0:1], zsel[:, 0:P], vec[0:ZR, ZSUM:ZSUM + 1], start=True, stop=True)
                pe.matmul(stat[0:ZR, 2:3], zsel[:, P:P + ZR], vec[0:ZR, ZSUM:ZSUM + 1], start=True, stop=True)
                statistics(G_OUT, vec[:, XSQ:XSQ + 1], stat[:, 1:2], gsel, P)
                statistics(G_Z, vec[:, XSQ:XSQ + 1], stat[0:ZR, 3:4], gsel, P).then_inc(p_stat, 1)
                pe.wait_ge(v_z, i + 1)
                for a in range(3):
                    pe.matmul(ps[0:48, BP + a, :], u_base[:, 2 * a, :] if a != AXC else u_base[:, 2, :], vc[0:ZR, :], start=True, stop=False)
                    pe.matmul(ps[0:48, BP + a, :], u_base[:, 2 * a + 1, :], vs[0:ZR, :], start=False, stop=True)
                for n, (k, g0) in enumerate(((0, 0), (1, 12), (2, 6), (3, 18))):
                    mm = pe.matmul(ps[0:48, BE, 0:6], u_base[:, k, :], gt[0:ZR, g0:g0 + 6], start=(n == 0), stop=(n == 3))
                mm.then_inc(p_u, 1)

                t0 = i * STRIPS
                u0 = i * (STRIPS // UNROLL)

                def turn(k, loads, t):
                    pe.wait_ge(x_loaded[k], loads * 48)
                    pe.wait_ge(xt_ready, t + FREE)
                    for q in range(4):
                        mm = pe.transpose(ps[:, BT, q * P:(q + 1) * P], chunk(q)(xin[:, k, :]), eye[:])
                    mm.then_inc(turned, 1)

                def hilbert(t):
                    pe.wait_ge(xt_ready, t + 1 + FREE)
                    pe.wait_ge(h_ready, t * 2 + FREE)
                    for q in range(4):
                        mm = pe.matmul(ps[:, BH + (q < 2), 0:HW_], xt[:, q, :], hil[:, q, :], start=(q % 2 == 0), stop=(q % 2 == 1))
                    mm.then_inc(h_done, 1)

                def mix(k, t):
                    o = k % 2
                    pe.wait_ge(w_ready, t + 1)
                    pe.wait_ge(g_ready, t + 1 + FREE)
                    pe.wait_ge(y_done, t + FREE)
                    for g in range(2):
                        sl = slice(HP * g, HP * g + HP)
                        for a in range(2):
                            mm = pe.matmul(ps[sl, BE, 0:6], wst[:, o, g, a, :], gst[:, o, g, 6 * a:6 * a + 6], start=(a == 0), stop=(a == 1))
                    mm.then_inc(e_done, 1)
                    pe.wait_ge(h_ready, t * 2 + 2 + FREE)
                    for a, done in ((AXB, pc_done), (AXC, ps_done)):
                        for g in range(2):
                            mm = pe.matmul(ps[HP * g:HP * g + HP, BP + a, :], wst[:, o, g, a, :], stack[:, o, g, :], start=True, stop=True)
                        mm.then_inc(done, 1)
                    for g in range(2):
                        pe.matmul(ps[HP * g:HP * g + HP, BP + AXS, :], strip[:, k, HP * g:HP * g + HP], u[:], start=True, stop=False)
                    for g in range(2):
                        mm = pe.matmul(ps[HP * g:HP * g + HP, BP + AXS, :], wst[:, o, g, AXS, :], stack[:, o, g, :], start=False, stop=True)
                    mm.then_inc(mixed, 1)

                pe.wait_ge(v_u, i * 2 + 2)
                turn(0, u0 + 1, t0)
                hilbert(t0)
                def project_next(s, uses, k):
                    if more:
                        pe.wait_ge(a_loaded[k], (u0 + STRIPS // UNROLL + uses + 1) * 32)
                        project(k, first=type(s) is int and s == 0)

                def step(s, uses, k):
                    turn((k + 1) % UNROLL, u0 + uses + 1 + (k + 1) // UNROLL, t0 + s + 1)
                    project_next(s, uses, k)
                    mix(k, t0 + s)
                    hilbert(t0 + s + 1)

                for s in range(UNROLL):
                    step(s, 0, s)
                with pe.Fori(1, STRIPS // UNROLL - 1) as j:
                    for k in range(UNROLL):
                        step(j * UNROLL + k, j, k)
                for s in range(STRIPS - UNROLL, STRIPS):
                    if s + 1 < STRIPS:
                        turn((s + 1) % UNROLL, u0 + s // UNROLL + 1, t0 + s + 1)
                    project_next(s, s // UNROLL, s % UNROLL)
                    mix(s % UNROLL, t0 + s)
                    if s + 1 < STRIPS:
                        hilbert(t0 + s + 1)

                pe.wait_ge(v_sums1, i + 1)
                pe.wait_ge(y_added, t0 + STRIPS + FREE)
                statistics(G_OUT, vec[:, ST1:ST1 + 2], stat[:, 0:2], gsel, P)
                statistics(G_PART, vec[:, ST1:ST1 + 2], stat[:, 2:4], gsel, P)
                pe.matmul(ps[:, BT, :], partner[:], acc, start=True, stop=True).then_inc(p_stat1, 1)
                pe.wait_ge(v_sums2, i + 1)
                statistics(G_OUT, vec[:, ST:ST + 2], stat[:, 0:2], gsel, P)
                statistics(G_CIN, vec[:, ST:ST + 2], stat[:, 4:6], gsel, P).then_inc(p_stat2, 1)

                for ph in range(2):
                    if ph == 1:
                        pe.wait_ge(v_sums3, i * 2 + 2)
                        statistics(G_CIN, vec[:, ST:ST + 2], stat[:, 0:2], gsel, P)
                        statistics(G_OUT, vec[:, ST:ST + 2], stat[:, 2:4], gsel, P).then_inc(p_stat3, 1)
                        pe.wait_ge(v_conv3, i + 1)
                        for t in range(TILES):
                            for m in range(2):
                                mm = pe.matmul(stat[TM * t:TM * (t + 1), 4:5], conv_s[:, m, :], vec[:, ZV:ZV + 1], start=(m == 0), stop=(m == 1))
                        mm.then_inc(p_bias3, 1)
                    with pe.Fori(0, STRIPS // UNROLL) as j:
                        for k in range(UNROLL):
                            slot = k % SLOTS
                            n = (i * 2 + ph) * STRIPS + j * UNROLL + k
                            pe.wait_ge(v_conv2 if ph == 0 else v_conv3, i + 1)
                            pe.wait_ge(c_loaded[slot], (n - k + k // SLOTS * SLOTS) * (32 // SLOTS) + 32)
                            pe.wait_ge(evicted, n + 1 - 4 + CONV_CREDIT)
                            for m, (q, first) in enumerate(((0, 0), (0, 1), (1, 1), (1, 2))):
                                for t in range(TILES):
                                    mm = pe.matmul(ps[TM * t:TM * (t + 1), 2 + k % 4, HALF * q:HALF * (q + 1)], conv_s[:, m, :],
                                                   cin[:, slot, t, first:first + HALF], start=(m % 2 == 0), stop=(m % 2 == 1))
                            mm.then_inc(convolved, 1)

            with pe.Fori(0, B - 1) as i:
                image(i, True)
            image(B - 1, False)


def kernel(x, L0_conv_w_real, L0_conv_w_imag, L0_conv_b_real, L0_conv_b_imag, L2_conv_W, L3_conv_weight):
    import numpy as _np
    import concourse.bacc as _bacc
    from concourse import mybir as _mybir
    from concourse.bass_utils import run_bass_kernel_spmd as _run

    a = [_np.asarray(v) for v in (L0_conv_w_real, L0_conv_w_imag, L0_conv_b_real, L0_conv_b_imag, L2_conv_W, L3_conv_weight)]
    arrays = {"x": _np.ascontiguousarray(x)}
    arrays.update(tables())
    arrays.update(placed(*a))
    nc = _bacc.Bacc("TRN2", target_bir_lowering=False, num_devices=1)
    args = {n: nc.dram_tensor(n, v.shape, _mybir.dt.from_np(v.dtype), kind="ExternalInput").ap() for n, v in arrays.items()}
    args["out"] = nc.dram_tensor("out", (B, C, N, N), _mybir.dt.float32, kind="ExternalOutput").ap()
    program(nc, **args)
    r = _run(nc, [arrays], core_ids=[0])
    return r.results[0]["out"]
```

```python
from contextlib import ExitStack

import numpy as np

import concourse.bass as bass
from concourse import mybir

F32 = mybir.dt.float32
ALU = mybir.AluOpType
ACT = mybir.ActivationFunctionType
AX_X = mybir.AxisListType.X

B, C, N = 8, 16, 512
P = 128
HP = P // 2
ROWS = 8
STRIPS = N // ROWS
UNROLL = 4
TILES = 4
TM = P // TILES
EPS = 1e-5
HALF = N // 2
NG = 24
HW_ = HALF + NG
AHEAD = 5 * UNROLL
COUTS = 4
STORES = 16 * STRIPS // COUTS
SLOTS2 = 8
SLOTS = 4
DOT_CREDIT = 2
THIRD_CREDIT = 16
THIRD_STRIPS = 9
DOTS, DVE_DOTS = 8, 5
OTHERS = DOTS - DVE_DOTS
FREE = 1
MIXED_CREDIT = STRIPS + UNROLL
CONV_CREDIT = 3 * UNROLL + 1
A_CREDIT = 4
ZERO_ROW = 96
AXB, AXC, AXS = 0, 1, 2
ZR = 96


def conv_in(layer, r, c, q):
    return (HP * q + C * r + c, 2 * C * r + 2 * c + q)[layer]


def tables():
    n = np.arange(N)
    th = 2 * np.pi * n / N
    cos, sin = np.cos(th), np.sin(th)
    split = np.concatenate([n[::2], n[1::2]])
    t = n[None, :] - n[:, None]
    odd = t % 2 != 0
    hil = np.where(odd, (2.0 / N) / np.tan(np.where(odd, np.pi * t / N, 1.0)), 0.0)
    ev = (n % 2 == 0).astype(float)
    od = 1 - ev
    z = 0 * ev
    g_xc = [z, z, z, z, -ev * cos / N, -od * cos / N]
    g_hc = [z, z, 2 / N * od, 2 / N * ev, od * sin / N, ev * sin / N]
    g_xs = [z, z, z, z, -ev * sin / N, -od * sin / N]
    g_hs = [-2 / N * od, -2 / N * ev, z, z, -od * cos / N, -ev * cos / N]
    g = np.stack(g_xc + g_xs + g_hc + g_hs, 1)
    hil_t = np.zeros((P, 4, HW_))
    for k in range(4):
        rows = split[k * P:(k + 1) * P]
        cols = n[1::2] if k < 2 else n[::2]
        hil_t[:, k, :HALF] = hil[rows][:, cols]
        hil_t[:, k, HALF:] = g[rows]
    mean_fix = np.zeros((P, NG))
    mean_fix[:, 12 + 2:12 + 4] = -1.0
    mean_fix[:, 18:20] = 1.0
    trig_cols = np.broadcast_to(np.stack([cos[split], sin[split]]), (P, 2, N))

    p = np.arange(P)
    ch, r4, half = p % C, (p % HP) // C, p // HP
    strip = np.zeros((STRIPS, P, P + 4 + HP))
    for s in range(STRIPS):
        row_out = ROWS * s + 4 * half + r4
        for k, f in enumerate((cos, sin, np.ones(N))):
            strip[s, C * k + ch, p] = f[row_out]
        strip[s, 64 + ch, p] = row_out == 0
        for gg in range(2):
            row = ROWS * s + 4 * gg + r4
            strip[s, :, P + 2 * gg] = cos[row]
            strip[s, :, P + 2 * gg + 1] = sin[row]
        for k, f in enumerate((np.ones(N), cos, sin)):
            strip[s, p, P + 4 + C * k + ch] = f[row_out] / N
    grp = ch // 2
    zc = np.arange(ZR) % 32
    dst = [grp, (p % 32) // 4, np.where(zc < C, zc // 2, -1), (grp + 4) % 8]
    scale = 1.0 / (2 * N * N)
    gsel = np.concatenate([(grp[:, None] == d[None, :]) * scale for d in dst], 1)
    partner = (ch[:, None] == (ch[None, :] + 8) % 16).astype(float)
    eye_mix = np.zeros((P, 2, 3, HP))
    for gg in range(2):
        for c in range(HP):
            eye_mix[HP * gg + c, gg, AXS, c] = 1.0
    eye_conv = np.zeros((P, 2, 4, TM))
    for l in range(2):
        for q in range(2):
            for r in range(2):
                for c in range(C):
                    eye_conv[conv_in(l, r + 1, c, q), l, 1 + q, C * r + c] = 1.0
    zsel = np.zeros((ZR, P + ZR))
    for k, d in enumerate((dst[0], dst[2])):
        zsel[:C, P * k:P * k + len(d)] = (np.arange(C)[:, None] // 2 == d[None, :]) / (2.0 * N)
    fold = np.zeros((P, ZR))
    for k in range(3):
        for c in range(C):
            fold[[C * k + c, HP + C * k + c], 32 * k + c] = 1.0
    small = np.zeros((P, 1))
    small[:C, 0] = 1.0
    bias_rows = np.zeros((P, 2, N))
    bias_rows[64:64 + C, 0] = (split == 0)
    bias_rows[64:64 + C, 1] = -hil[0][split]
    f = lambda a: np.ascontiguousarray(a, dtype=np.float32)
    return {
        "t_eye": f(np.eye(P)), "t_hil": f(hil_t), "t_fix": f(mean_fix), "t_trig": f(trig_cols),
        "t_strip": f(strip), "t_gsel": f(gsel), "t_zsel": f(zsel), "t_fold": f(fold), "t_partner": f(partner),
        "t_eye_mix": f(eye_mix), "t_eye_conv": f(eye_conv), "t_small": f(small), "t_bias": f(bias_rows),
    }


def placed(w_real, w_imag, b_real, b_imag, w2, w3):
    w = np.stack([w_real, w_imag])[:, :, :, ::-1, ::-1]
    w = w.transpose(1, 3, 4, 0, 2)
    mix = np.zeros((P, 3, 3, 2, HP), np.float32)
    uw = np.zeros((ZR, 3, 3, 2, C), np.float32)
    for c in range(C):
        for half in range(2):
            for r in range(4):
                mix[HP * half + C * r + c, :, :, :, C * r:C * r + C] = w[c]
        for k in range(3):
            uw[32 * k + c] = w[c]
    bias = np.zeros((P, 2), np.float32)
    bias[64:64 + C, 0] = b_real
    bias[64:64 + C, 1] = b_imag
    taps = (((1, 0),), ((0, 1), (1, 2)), ((0, 0), (1, 1)), ((0, 2),))
    convs = np.zeros((P, 2, 4, TM), np.float32)
    for l, wt in enumerate((w2, w3.reshape(C, C, 3, 3))):
        for m, pairs in enumerate(taps):
            for q, kw in pairs:
                for r in range(2):
                    for kh in range(3):
                        for c in range(C):
                            convs[conv_in(l, r + kh, c, q), l, m, C * r:C * r + C] = wt[:, c, kh, kw]
    return {"w_mix": mix, "w_u": uw, "w_bias": bias, "w_conv": convs}


class Steps:

    def __init__(self, eng, sem, base):
        self.eng, self.sem, self.base, self.n = eng, sem, base, 0

    def did(self, ins):
        ins.then_inc(self.sem, 1)
        self.n += 1

    def settle(self):
        self.eng.wait_ge(self.sem, self.base + self.n)

    def then(self, ins):
        self.did(ins)
        self.settle()


DVE_B = 15
MOMENTS = 5
Z_STEPS = 31
DVE_PREPS = 52


def program(nc, x, t_eye, t_hil, t_fix, t_trig, t_strip, t_gsel, t_zsel, t_fold, t_partner, t_eye_mix,
            t_eye_conv, t_small, t_bias, w_mix, w_u, w_bias, w_conv, out):
    with ExitStack() as ctx:
        def sb(name, *shape):
            return ctx.enter_context(nc.sbuf_tensor(name, list(shape), F32))

        def sem(name):
            return ctx.enter_context(nc.semaphore(name))

        in3 = nc.dram_tensor("in3", [N + 2, C, N], F32).ap()

        ps = ctx.enter_context(nc.psum_tensor("ps", [P, 8, 512], F32))
        BU = (0, 1, 7)
        BT, BH, BP, BE, BZ = 0, 1, 3, 6, 7
        stat = ps[:, BE, 16:32]

        eye = sb("eye", P, P)
        hil = sb("hil", P, 4, HW_)
        fix = sb("fix", P, NG)
        trig = sb("trig", P, 2, N)
        gsel = sb("gsel", P, 128 + 128 + ZR + 128)
        fold = sb("fold", P, ZR)
        zz = sb("zz", P, N)
        zsel = sb("zsel", ZR, P + ZR)
        partner = sb("partner", P, P)
        small = sb("small", P, 1)
        bias_w = sb("bias_w", P, 2)
        mix_base = sb("mix_base", P, 3, 2, 3, HP)
        mix_s = sb("mix_s", P, 3, 2, 3, HP)
        eye_mix = sb("eye_mix", P, 2, 3, HP)
        u_base = sb("u_base", ZR, 6, 48)
        conv_w = sb("conv_w", P, 2, 4, TM)
        conv_eye = sb("conv_eye", P, 2, 4, TM)
        conv_s = sb("conv_s", P, 4, TM)
        x1 = sb("x1", P, STRIPS, N)
        xin = sb("xin", P, UNROLL, N)
        cout = xin
        shared = sb("shared", P, SLOTS2 * TILES * (HALF + 2))
        cin = shared[:].rearrange("p (k t w) -> p k t w", k=SLOTS2, t=TILES)
        taken = 0

        def part(pattern, **dims):
            nonlocal taken
            size = int(np.prod(list(dims.values())))
            taken += size
            assert taken <= SLOTS2 * TILES * (HALF + 2)
            return shared[:, taken - size:taken].rearrange(pattern, **dims)

        stack = part("p (b g w) -> p b g w", b=2, g=2, w=N)
        xa = part("p (k w) -> p k w", k=UNROLL, w=N)
        xt = part("p (a b) -> p a b", a=4, b=P)
        product = shared[:, 0:OTHERS * N].rearrange("p (b w) -> p b w", b=OTHERS)
        assert taken >= SLOTS * TILES * (HALF + 2)
        vy = part("p (q w) -> p (q w)", q=2, w=HALF)
        junk = part("p (q w) -> p (q w)", q=2, w=HALF)
        acc = part("p (q w) -> p (q w)", q=2, w=HALF)
        wst = part("p (o g a m) -> p o g a m", o=2, g=2, a=3, m=HP)
        zt = part("p (a b) -> p a b", a=4, b=ZR)
        strip = part("p (k w) -> p k w", k=UNROLL, w=P + 4 + HP)
        gp = sb("gp", P, 2, NG)
        gt = sb("gt", P, NG)
        gst = sb("gst", P, 2, 2, 12)
        ev_e = sb("ev_e", P, 2, 6)
        work = sb("work", P, 2, N)
        vc, vs = (work[:, k, :] for k in range(2))
        colv = vs
        u = sb("u", P, N)
        cols = sb("cols", P, 8, STRIPS)
        vec = sb("vec", P, 32)
        tick = sb("tick", P, 2)
        red = sb("red", P, DOTS)

        s_const = sem("constants_loaded")
        s_setup = sem("setup_steps")
        s_based = sem("setup_done")
        s_pool = sem("pool_zeroed")
        a_loaded = [sem(f"a_loaded{k}") for k in range(UNROLL)]
        a_table = [sem(f"a_table{k}") for k in range(UNROLL)]
        a_squared, a_projected = sem("a_squared"), sem("a_projected")
        z_steps = sem("z_steps")
        v_xsq = sem("x_squares")
        d_prep, v_var, a_root = sem("dve_prep_steps"), sem("var_ready"), sem("root_ready")
        a_kept, p_zt = sem("column_sums_kept"), sem("pe_zt")
        p_stat, p_zin, p_zh, p_u = sem("pe_stat"), sem("pe_zin"), sem("pe_zh"), sem("pe_u")
        v_sums0, v_zt, v_scaled, v_z, v_u = sem("sums0"), sem("zt_ready"), sem("mix_scaled"), sem("z_ready"), sem("u_ready")
        x_loaded = [sem(f"x_loaded{k}") for k in range(UNROLL)]
        turned, xt_ready, h_done, h_ready = sem("turned"), sem("xt_ready"), sem("h_done"), sem("h_ready")
        g_taken, g_ready, w_ready, e_done = sem("g_taken"), sem("g_ready"), sem("w_ready"), sem("e_done")
        pc_done, ps_done, mixed = sem("pc_done"), sem("ps_done"), sem("mixed")
        b_steps, y_done, y_squared, y_added = sem("b_steps"), sem("y_done"), sem("y_squared"), sem("y_added")
        acc_zero = sem("acc_zeroed")
        v_sums1, p_stat1, v_colv = sem("sums1"), sem("pe_stat1"), sem("colv_ready")
        dotted, dots_kept = sem("dotted"), sem("dots_kept")
        multiplied, a_dotted = sem("multiplied"), sem("dotted_by_act")
        v_sums2, p_stat2, v_conv2 = sem("sums2"), sem("pe_stat2"), sem("conv2_weights")
        gated, v_gates = sem("gated"), sem("gates_ready")
        c_loaded = [sem(f"c_loaded{k}") for k in range(SLOTS)]
        c_stored = [sem(f"c_stored{h}") for h in range(COUTS // 2)]
        e_loaded = [sem(f"layer2_edges_loaded{e}") for e in range(3)]
        edges_due = sem("edges_due")
        d_loaded = [sem(f"layer2_loaded{e}") for e in range(3)]
        third_ready = sem("third_part_ready")
        d_top, d_bottom = sem("row_above_loaded"), sem("row_below_loaded")
        v_pad3, pad3_stored = sem("pad3_ready"), sem("pad_rows3_stored")
        convolved, evicted, c_squared, c_reduced = sem("convolved"), sem("evicted"), sem("c_squared"), sem("c_reduced")
        v_sums3, p_stat3, v_conv3, p_bias3, v_bias3 = sem("sums3"), sem("pe_stat3"), sem("conv3_weights"), sem("pe_bias3"), sem("bias3")

        block = ctx.enter_context(nc.Block())

        MEAN, RS, NEGM, VAR, MZ, MEANP, SV, BIAS3 = 0, 1, 2, 3, 5, 6, 7, 9
        ST, ST1, CM, XSQ, ZSUM, ZV = 12, 14, 16, 17, 18, 20

        def v1(k, p0=0, p1=P):
            return vec[p0:p1, k:k + 1]

        assert STRIPS % UNROLL == 0 and UNROLL == SLOTS == COUTS and SLOTS2 == 2 * UNROLL

        G_OUT, G_CIN, G_Z, G_PART = (0, 128), (128, 256), (256, 256 + ZR), (256 + ZR, 384 + ZR)

        split_in = lambda a: a.rearrange("p (w q) -> p q w", q=2)
        halves = lambda a: a.rearrange("p (q w) -> p q w", q=2)

        GROUPS = STRIPS // UNROLL

        RING = [cin[:, 0:UNROLL], cin[:, UNROLL:2 * UNROLL],
                x1[:, 0:THIRD_STRIPS, :].rearrange("p a b -> p (a b)")[:, 0:UNROLL * TILES * (HALF + 2)].rearrange(
                    "p (k t w) -> p k t w", k=UNROLL, t=TILES)]
        USES = (6, 5, 5)
        TURN = (2, 1, 0)
        TURNS = (GROUPS - 4) // 3
        assert GROUPS == 4 + 3 * TURNS

        def in_groups(eng, group):
            group(0, 0, 0)
            group(1, 1, 0)
            group(2, 0, 1)
            with eng.Fori(0, TURNS) as jj:
                for m, e in enumerate(TURN):
                    group(jj * 3 + 3 + m, e, jj + (2, 1, 0)[e])
            group(GROUPS - 1, 2, TURNS)

        def wait_group(eng, i, g):
            due = i * (2 * STRIPS) + (3 if type(g) is int and g == 2 else g) * UNROLL + UNROLL + 1
            assert CONV_CREDIT == 3 * UNROLL + 1
            if type(g) is not int:
                eng.wait_ge(third_ready, i * (2 * STRIPS) + THIRD_CREDIT + 1)
            eng.wait_ge(convolved, due)
            eng.wait_ge(gated, due)

        def copy_rows(eng, loaded, g, e, t, r, rows, p0, shift=0, count=UNROLL, skip=0):
            for q in range(2):
                d0 = HP * q + C * r
                eng.dma_start(RING[e][d0:d0 + C * rows, skip:skip + count, t, 1:HALF + 1],
                              x1[p0:p0 + C * rows, bass.ds(g * UNROLL + shift + skip, count), HALF * q:HALF * (q + 1)]).then_inc(loaded[e], 16)

        def load_rows(eng, i, g, e):
            wait_group(eng, i, g)
            copy_rows(eng, d_loaded, g, e, 0, 1, 3, 0)
            copy_rows(eng, d_loaded, g, e, 1, 0, 4, C)
            copy_rows(eng, d_loaded, g, e, 2, 0, 4, 3 * C)
            copy_rows(eng, d_loaded, g, e, 3, 0, 3, 5 * C)

        def load_edges(eng, i, g, e):
            top, bottom = (type(g) is int and g == 0), (type(g) is int and g == GROUPS - 1)
            wait_group(eng, i, g)
            eng.wait_ge(edges_due, i * GROUPS + g + 1)
            eng.tensor_tensor(tick[:, 0:1], tick[:, 1:2], tick[:, 1:2], ALU.add).then_inc(edges_due, 1)
            for at_end, slot, t, r, done in ((top, 0, 0, 0, d_top), (bottom, UNROLL - 1, 3, 3, d_bottom)):
                if at_end:
                    for q in range(2):
                        d0 = HP * q + C * r
                        eng.dma_start(RING[e][d0:d0 + C, slot, t, 1:HALF + 1], u[ZERO_ROW:ZERO_ROW + C, HALF * q:HALF * (q + 1)]).then_inc(done, 16)
            copy_rows(eng, e_loaded, g, e, 0, 0, 1, P - C, -1, UNROLL - top, int(top))
            copy_rows(eng, e_loaded, g, e, 3, 3, 1, 0, 1, UNROLL - bottom)

        @block.sync
        def _(sp):
            for dst, src in ((eye[:], t_eye), (hil[:], t_hil), (fix[:], t_fix), (trig[:], t_trig),
                             (gsel[:], t_gsel), (zsel[:], t_zsel), (fold[:], t_fold), (conv_w[:], w_conv), (conv_eye[:], t_eye_conv), (partner[:], t_partner),
                             (small[:], t_small), (bias_w[:], w_bias), (eye_mix[:], t_eye_mix),
                             (x1[:, 0:3, :].rearrange("p a b -> p (a b)")[:, 0:1152], w_mix.rearrange("p a b c d -> p (a b c d)")),
                             (x1[0:ZR, 3:4, 0:288].rearrange("p a b -> p (a b)"), w_u.rearrange("p a b c d -> p (a b c d)")),
                             (x1[:, 4:6, :], t_bias)):
                sp.dma_start(dst, src).then_inc(s_const, 16)

            def load_x(i, s, slot, dst, loaded):
                for g in range(2):
                    src = x[i].rearrange("c (s g r) w -> s g r c w", g=2, r=4)[s, g]
                    sp.dma_start(dst[HP * (1 - g):HP * (2 - g), slot, :], src).then_inc(loaded[slot], 16)

            for h in range(COUTS // 2):
                sp.sem_inc(c_stored[h], FREE)

            def load_next(image, s, t, k):
                sp.wait_ge(a_squared, t + 1)
                sp.wait_ge(a_projected, t + 1)
                sp.dma_start(xa[:, k, :], x[image].rearrange("c (s r) w -> s r c w", r=ROWS)[s]).then_inc(a_loaded[k], 16)

            with sp.Fori(0, STRIPS // UNROLL) as j:
                for k in range(UNROLL):
                    s = j * UNROLL + k
                    load_next(0, s, s, k)
                    sp.dma_start(strip[:, k, :], t_strip[s]).then_inc(a_table[k], 16)

            def image(i, more):
                with sp.Fori(0, STRIPS // UNROLL) as j:
                    for k in range(UNROLL):
                        s = j * UNROLL + k
                        t = i * STRIPS + s
                        sp.wait_ge(c_stored[k // 2], i * (3 * STORES) + FREE)
                        sp.wait_ge(a_projected, t + STRIPS + 1 if more else B * STRIPS + A_CREDIT)
                        sp.wait_ge(mixed, t + 1 - UNROLL + MIXED_CREDIT)
                        load_x(i, s, k, xin, x_loaded)
                        sp.dma_start(strip[:, k, :], t_strip[s]).then_inc(x_loaded[k], 16)
                        if more:
                            sp.wait_ge(convolved, i * (2 * STRIPS) + CONV_CREDIT)
                            load_next(i + 1, s, t + STRIPS, k)
                in_groups(sp, lambda g, e, use: load_rows(sp, i, g, e))

                sp.wait_ge(v_pad3, i + 1)
                for h in range(COUTS // 2):
                    sp.wait_ge(c_stored[h], i * (3 * STORES) + STORES + FREE)
                for row in (0, N + 1):
                    sp.dma_start(in3[row], vc[0:C, :]).then_inc(pad3_stored, 16)
                with sp.Fori(0, STRIPS // UNROLL) as j:
                    for k in range(UNROLL):
                        s = j * UNROLL + k
                        views = [in3[2 * h:2 * h + ((N - 2 * h + 2) // ROWS) * ROWS].rearrange(
                            "(s a r) c (q w) -> s (r c q) a w", a=2, r=4, q=2) for h in range(2)]
                        sp.wait_ge(pad3_stored, (i + 1) * 32)
                        sp.wait_ge(v_conv3, i + 1)
                        sp.wait_ge(convolved, (i * 2 + 1) * STRIPS + s + 1 - SLOTS + CONV_CREDIT)
                        for h in range(2):
                            sp.dma_start(cin[:, k].rearrange("p (a h) w -> p h a w", h=2)[:, h, :, 1:HALF + 1],
                                         views[h][s]).then_inc(c_loaded[k], 16)
            with sp.Fori(0, B - 1) as i:
                image(i, True)
            image(B - 1, False)
            for h in range(COUTS // 2):
                sp.wait_ge(c_stored[h], B * (3 * STORES) + FREE)

        @block.gpsimd
        def _(pool):
            pool.sem_inc(y_added, FREE)
            nc.gpsimd.memset(u[:], 0.0).then_inc(s_pool, 1)
            nc.gpsimd.memset(u_base[:], 0.0).then_inc(s_pool, 1)
            nc.gpsimd.memset(tick[:], 0.0).then_inc(edges_due, 1)
            with pool.Fori(0, B) as i:
                with pool.Fori(0, STRIPS) as s:
                    t = i * STRIPS + s
                    pool.wait_ge(acc_zero, i + 1)
                    pool.wait_ge(y_done, t + 1 + FREE)
                    pool.wait_ge(y_added, t + FREE)
                    nc.gpsimd.tensor_tensor(acc, acc, x1[:, bass.ds(s, 1), :].rearrange("p a w -> p (a w)"), ALU.add).then_inc(y_added, 1)
                with pool.Fori(0, STRIPS // DOTS) as j:
                    for b in range(OTHERS):
                        n = (i * (STRIPS // DOTS) + j) * OTHERS + b
                        pool.wait_ge(v_colv, i + 1)
                        pool.wait_ge(a_dotted, n + 1)
                        nc.gpsimd.tensor_tensor(product[:, b, :], x1[:, bass.ds(j * DOTS + DVE_DOTS + b, 1), :].rearrange("p a w -> p (a w)"),
                                                colv, ALU.mult).then_inc(multiplied, 1)
                in_groups(pool, lambda g, e, use: load_edges(nc.gpsimd, i, g, e))

        @block.scalar
        def _(act):
            act.sem_inc(a_squared, A_CREDIT)
            act.sem_inc(a_dotted, OTHERS)
            act.sem_inc(evicted, CONV_CREDIT)
            for signal in (y_squared, xt_ready, h_ready):
                act.sem_inc(signal, FREE)
            def square_next(s, t, loads, k):
                act.wait_ge(a_loaded[k], loads * 16)
                nc.scalar.activation(junk, xa[:, k, :], ACT.Square, accum_out=cols[:, 6, bass.ds(s, 1)]).then_inc(a_squared, 1)

            with act.Fori(0, STRIPS // UNROLL) as j:
                for k in range(UNROLL):
                    act.wait_ge(a_squared, j * UNROLL + k + A_CREDIT)
                    square_next(j * UNROLL + k, j * UNROLL + k, j + 1, k)

            def keep(n):
                act.wait_ge(a_projected, n * STRIPS + STRIPS + A_CREDIT)
                nc.scalar.activation(halves(zz[:]), split_in(ps[:, BZ, :]), ACT.Identity).then_inc(a_kept, 1)

            keep(0)

            def root(i, n, dst, p1=P):
                act.wait_ge(v_var, i * MOMENTS + n + 1)
                nc.scalar.activation(v1(dst + 1, 0, p1), v1(dst + 3, 0, p1), ACT.Sqrt).then_inc(a_root, 1)

            root(0, 0, 0)
            root(0, 1, ZV, ZR)

            def image(i, more):
                act.wait_ge(v_scaled, i + 1)

                def bring(t, loads, k):
                    act.wait_ge(x_loaded[k], loads * 48)
                    act.wait_ge(mixed, t - 1 + MIXED_CREDIT)
                    b = k % 2
                    nc.scalar.activation(halves(stack[0:HP, b, 0, :]), split_in(xin[HP:P, k, :]), ACT.Identity,
                                         bias=v1(NEGM, HP, P))
                    nc.scalar.activation(halves(stack[HP:P, b, 1, :]), split_in(xin[0:HP, k, :]), ACT.Identity,
                                         bias=v1(NEGM, 0, HP))
                    act.wait_ge(turned, t + 1)
                    act.wait_ge(h_done, t + FREE)
                    nc.scalar.activation(xt.rearrange("p a b -> p (a b)"), ps[:, BT, :], ACT.Identity).then_inc(xt_ready, 1)
                    act.wait_ge(h_done, t + 1 + FREE)
                    act.wait_ge(g_ready, t + FREE)
                    nc.scalar.activation(gp[:], ps[:, BH:BH + 2, HALF:HW_], ACT.Identity).then_inc(g_taken, 1)
                    nc.scalar.activation(halves(stack[HP:P, b, 0, :]), ps[HP:P, BH:BH + 2, 0:HALF], ACT.Identity).then_inc(h_ready, 1)
                    nc.scalar.activation(halves(stack[0:HP, b, 1, :]), ps[0:HP, BH:BH + 2, 0:HALF], ACT.Identity).then_inc(h_ready, 1)

                def square(t, s):
                    act.wait_ge(y_done, t + 1 + FREE)
                    act.wait_ge(y_squared, t + FREE)
                    act.wait_ge(a_squared, t + STRIPS + A_CREDIT if more else B * STRIPS + A_CREDIT)
                    nc.scalar.activation(junk, x1[:, bass.ds(s, 1), :].rearrange("p a w -> p (a w)"), ACT.Square,
                                         accum_out=cols[:, 1, bass.ds(s, 1)]).then_inc(y_squared, 1)

                u0 = i * (STRIPS // UNROLL)
                t0 = i * STRIPS
                bring(t0, u0 + 1, 0)
                with act.Fori(0, STRIPS // UNROLL - 1) as j:
                    for k in range(UNROLL):
                        s = j * UNROLL + k
                        bring(t0 + s + 1, u0 + j + 1 + (k + 1) // UNROLL, (k + 1) % UNROLL)
                        square(t0 + s, s)
                        if more:
                            act.wait_ge(y_squared, t0 + s + 1 + FREE)
                            square_next(s, t0 + STRIPS + s, u0 + STRIPS // UNROLL + j + 1, k)
                for s in range(STRIPS - UNROLL, STRIPS):
                    if s + 1 < STRIPS:
                        bring(t0 + s + 1, u0 + s // UNROLL + 1, (s + 1) % UNROLL)
                    square(t0 + s, s)
                    if more:
                        act.wait_ge(y_squared, t0 + s + 1 + FREE)
                        square_next(s, t0 + STRIPS + s, u0 + STRIPS // UNROLL + s // UNROLL + 1, s % UNROLL)

                if more:
                    keep(i + 1)
                act.wait_ge(y_squared, t0 + STRIPS + FREE)
                if more:
                    act.wait_ge(a_squared, t0 + 2 * STRIPS + A_CREDIT)
                root(i, 2, 0)
                with act.Fori(0, STRIPS // DOTS) as j:
                    for b in range(OTHERS):
                        n = (i * (STRIPS // DOTS) + j) * OTHERS + b
                        act.wait_ge(multiplied, n + 1)
                        act.wait_ge(a_dotted, n + OTHERS)
                        nc.scalar.activation(junk, product[:, b, :], ACT.Identity,
                                             accum_out=cols[:, 2, bass.ds(j * DOTS + DVE_DOTS + b, 1)]).then_inc(a_dotted, 1)
                root(i, 3, ZV)
                for ph in range(2):
                    if ph == 1:
                        root(i, 4, ZV)
                    act.wait_ge(v_gates if ph == 0 else v_bias3, i + 1)
                    if ph == 0:
                        def gate(s):
                            xs = x1[:, bass.ds(s, 1), :].rearrange("p a w -> p (a w)")
                            nc.scalar.activation(xs, xs, ACT.Identity, scale=cols[:, 4, bass.ds(s, 1)],
                                                 bias=cols[:, 5, bass.ds(s, 1)]).then_inc(gated, 1)
                        for k in range(AHEAD):
                            gate(k)

                    def evict(j, more):
                        for k in range(UNROLL):
                            s = j * UNROLL + k
                            n = (i * 2 + ph) * STRIPS + s
                            if more:
                                gate(s + AHEAD)
                            o = k % COUTS
                            act.wait_ge(convolved, n + 1 + CONV_CREDIT)
                            act.wait_ge(c_stored[o // 2], i * (3 * STORES) + (j * 16 if ph == 0 else STORES + j * 32) + FREE)
                            if ph == 0:
                                act.wait_ge(c_squared, i * STRIPS + s + 1 - COUTS + CONV_CREDIT)
                                nc.scalar.activation(cout[:, o, :], ps[:, 2 + k % 4, :], ACT.Identity, bias=v1(MEANP),
                                                     accum_out=cols[:, 2, bass.ds(s, 1)]).then_inc(evicted, 1)
                            else:
                                nc.scalar.activation(cout[:, o, :].rearrange("p (w q) -> p q w", q=2), halves(ps[:, 2 + k % 4, :]),
                                                     ACT.Identity, bias=v1(BIAS3)).then_inc(evicted, 1)
                            if ph == 1:
                                act.wait_ge(evicted, n + 1 + CONV_CREDIT)
                                act.dma_start(out[i].rearrange("c (s r) w -> s r c w", r=ROWS)[s], cout[:, o, :]).then_inc(c_stored[o // 2], 16)
                            elif k % 2:
                                act.wait_ge(evicted, n + 1 + CONV_CREDIT)
                                dst = in3[1:N + 1].rearrange("(a h s r) c w -> a h (r c) s w", r=ROWS, s=2, h=2)
                                act.dma_start(dst[j, k // 2], cout[:, o - 1:o + 1, :]).then_inc(c_stored[o // 2], 16)

                    ahead = AHEAD // UNROLL if ph == 0 else 0
                    first = 0
                    if ph == 1 and more:
                        first = 10
                        with act.Fori(0, first) as j:
                            evict(j, False)
                        root(i + 1, 0, 0)
                        root(i + 1, 1, ZV, ZR)
                    with act.Fori(first, STRIPS // UNROLL - ahead) as j:
                        evict(j, ph == 0)
                    if ph == 0:
                        act.wait_ge(gated, i * (2 * STRIPS) + STRIPS)
                        act.sem_inc(gated, STRIPS)
                    for j in range(STRIPS // UNROLL - ahead, STRIPS // UNROLL):
                        evict(j, False)

            with act.Fori(0, B - 1) as i:
                image(i, True)
            image(B - 1, False)

        @block.vector
        def _(dve):
            V = nc.vector
            dve.sem_inc(c_squared, CONV_CREDIT)
            dve.sem_inc(dotted, DOT_CREDIT)
            dve.sem_inc(third_ready, THIRD_CREDIT)
            for signal in (g_ready, y_done, dots_kept, c_reduced):
                dve.sem_inc(signal, FREE)
            st = Steps(dve, s_setup, 0)
            dve.wait_ge(s_const, 16 * 16)
            dve.wait_ge(s_pool, 2)
            wm = x1[:, 0:3, :].rearrange("p a b -> p (a b)")[:, 0:1152].rearrange("p (a b c d) -> p a b c d", a=3, b=3, c=2)
            wu = x1[0:ZR, 3:4, 0:288].rearrange("p a b -> p (a b)").rearrange("p (a b c d) -> p a b c d", a=3, b=3, c=2)
            tmp = x1[:, 8:16, :].rearrange("p a b -> p (a b)")
            q3 = tmp[:, 0:1152].rearrange("p (j b c d) -> p j b c d", j=3, b=3, c=2)
            pm = tmp[:, 1152:1152 + 768].rearrange("p (j f c d) -> p j f c d", j=3, f=2, c=2)
            fl = lambda a: a.rearrange("p b c d -> p (b c d)")
            st.did(V.tensor_copy(fl(q3[:, 0]), fl(wm[:, 1])))
            st.did(V.tensor_tensor(fl(q3[:, 1]), fl(wm[:, 2]), fl(wm[:, 0]), ALU.add))
            st.then(V.tensor_tensor(fl(q3[:, 2]), fl(wm[:, 2]), fl(wm[:, 0]), ALU.subtract))
            for j in range(3):
                for f, op in enumerate((ALU.add, ALU.subtract)):
                    st.did(V.tensor_tensor(pm[:, j, f], q3[:, j, 2], q3[:, j, 0], op))
            st.settle()
            for j in range(3):
                re, im = ((1, 0), (1, 1)) if j < 2 else ((1, 1), (-1, 0))
                for g in range(2):
                    for kind in range(2):
                        h0 = HP * (g ^ kind)
                        sl = slice(h0, h0 + HP)
                        for a in range(3):
                            which, sgn = ((re, 1), (im, -1)) [kind] if a != AXC else ((im, 1), (re, 1))[kind]
                            src = q3[sl, j, 1, which[1]] if a == AXS else pm[sl, j, a, which[1]]
                            st.did(V.tensor_scalar(mix_base[sl, j, g, a, :], src, float(which[0] * sgn), None, ALU.mult))
            pu = tmp[0:ZR, 2048:2048 + 192].rearrange("p (k f c d) -> p k f c d", k=3, f=2, c=2)
            for d1 in (0, 2):
                for f, op in enumerate((ALU.add, ALU.subtract)):
                    st.did(V.tensor_tensor(pu[:, d1, f], wu[:, d1, 2], wu[:, d1, 0], op))
            st.settle()
            for z, blk, d1, re, im in ((0, 0, 2, (1, 0), (1, 1)), (0, 1, 2, (1, 1), (-1, 0)),
                                       (1, 2, 0, (1, 0), (1, 1)), (2, 2, 0, (-1, 1), (1, 0))):
                sl = slice(32 * z, 32 * z + C)
                for k, (which, sgn, f) in enumerate(((re, 1, 0), (im, -1, 0), (im, 1, 1), (re, 1, 1), (re, 1, 2), (im, -1, 2))):
                    src = wu[sl, d1, 1, which[1]] if f == 2 else pu[sl, d1, f, which[1]]
                    st.did(V.tensor_scalar(u_base[sl, k, 16 * blk:16 * blk + 16], src, float(-which[0] * sgn), None, ALU.mult))
            sl = slice(64, 64 + C)
            br = x1[:, 4:6, :]
            st.then(V.tensor_scalar(u[sl, :], br[sl, 0, :], bias_w[sl, 0:1], None, ALU.mult))
            V.scalar_tensor_tensor(u[sl, :], br[sl, 1, :], bias_w[sl, 1:2], u[sl, :], ALU.mult, ALU.add).then_inc(s_based, 1)
            dve.wait_ge(s_based, 1)

            def moments(i, c, n, src, dst, p1=P):
                variance(c, src, dst, p1)
                inverse_root(i, c, n, dst, p1)

            def variance(c, src, dst, p1=P):
                mean, rs, neg, var = (v1(dst + k, 0, p1) for k in (0, 1, 2, 3))
                c.then(V.tensor_copy(vec[0:p1, dst:dst + 2], src))
                c.did(V.tensor_scalar(neg, mean, -1.0, None, ALU.mult))
                c.then(V.tensor_tensor(var, mean, mean, ALU.mult))
                c.then(V.tensor_tensor(var, rs, var, ALU.subtract))
                V.tensor_scalar(var, var, 0.0, EPS, ALU.max, ALU.add).then_inc(v_var, 1)

            def inverse_root(i, c, n, dst, p1=P):
                rs, var, t = (v1(dst + k, 0, p1) for k in (1, 3, 4))
                dve.wait_ge(a_root, i * MOMENTS + n + 1)
                c.then(V.reciprocal(rs, rs))
                c.then(V.tensor_tensor(t, rs, rs, ALU.mult))
                c.then(V.tensor_tensor(t, t, var, ALU.mult))
                c.then(V.tensor_scalar(t, t, -0.5, 1.5, ALU.mult, ALU.add))
                c.then(V.tensor_tensor(rs, rs, t, ALU.mult))

            def take_next(n):
                dve.wait_ge(a_squared, n * STRIPS + STRIPS + A_CREDIT)
                V.tensor_reduce(v1(XSQ), cols[:, 6, :], AX_X, ALU.add).then_inc(v_xsq, 1)

            take_next(0)

            def prepare(n):
                c = Steps(dve, z_steps, n * Z_STEPS)
                dve.wait_ge(p_zt, n + 1)
                V.tensor_copy(zt.rearrange("p a b -> p (a b)"), ps[:, BZ, 0:4 * ZR]).then_inc(v_zt, 1)
                dve.wait_ge(p_zin, n + 1)
                V.tensor_reduce(v1(ZSUM, 0, ZR), ps[0:ZR, BT, :], AX_X, ALU.add).then_inc(v_sums0, 1)
                dve.wait_ge(p_stat, n + 1)
                moments(n, c, 0, stat[:, 0:2], 0)
                moments(n, c, 1, stat[0:ZR, 2:4], ZV, ZR)
                c.then(V.tensor_tensor(v1(MZ, 0, ZR), v1(ZV, 0, ZR), small[0:ZR, 0:1], ALU.mult))
                flat = lambda a: a.rearrange("p g a o -> p (g a o)")
                for jj in (1, 2):
                    c.did(V.tensor_scalar(flat(mix_s[:, jj]), flat(mix_base[:, jj]), v1(1), None, ALU.mult))
                V.scalar_tensor_tensor(flat(mix_s[:, 0]), flat(mix_base[:, 0]), v1(1), flat(eye_mix[:]), ALU.mult, ALU.add).then_inc(v_scaled, 1)
                dve.wait_ge(v_scaled, n + 1)
                zs, zhs, zg = vc, vs, gt
                if type(n) is not int:
                    dve.wait_ge(pad3_stored, n * 32)
                c.did(V.tensor_scalar(zs[0:ZR, :], ps[0:ZR, BT, :], v1(MZ, 0, ZR), v1(ZV + 1, 0, ZR), ALU.subtract, ALU.mult))
                dve.wait_ge(p_zh, n + 1)
                c.did(V.tensor_scalar(halves(zhs[0:ZR, :]), ps[0:ZR, BH, :].rearrange("p (q w) -> p q w", q=2), v1(ZV + 1, 0, ZR), None, ALU.mult))
                c.then(V.scalar_tensor_tensor(zg[0:ZR, :], fix[0:ZR, :], v1(MZ, 0, ZR), ps[0:ZR, BZ, 0:NG], ALU.mult, ALU.add))
                c.then(V.tensor_tensor(zg[0:ZR, :], zg[0:ZR, :], ps[0:ZR, BZ, NG:2 * NG], ALU.add))
                V.tensor_scalar(zg[0:ZR, :], zg[0:ZR, :], v1(ZV + 1, 0, ZR), None, ALU.mult).then_inc(v_z, 1)
                dve.wait_ge(p_u, n + 1)
                c.then(V.tensor_copy(ev_e[0:48, 0, :], ps[0:48, BE, 0:6]))
                for q in range(2):
                    w = slice(HALF * q, HALF * (q + 1))
                    c.did(V.scalar_tensor_tensor(vy[0:48, w], ps[0:48, BU[AXB], w], ev_e[0:48, 0, q:q + 1], trig[0:48, 0, w], ALU.add, ALU.mult))
                    c.did(V.scalar_tensor_tensor(u[0:48, w], ps[0:48, BU[AXC], w], ev_e[0:48, 0, 2 + q:3 + q], trig[0:48, 1, w], ALU.add, ALU.mult))
                c.settle()
                c.then(V.tensor_tensor(vy[0:48, :], vy[0:48, :], u[0:48, :], ALU.add))
                for q in range(2):
                    w = slice(HALF * q, HALF * (q + 1))
                    V.scalar_tensor_tensor(u[0:48, w], ps[0:48, BU[AXS], w], ev_e[0:48, 0, 4 + q:5 + q], vy[0:48, w], ALU.add, ALU.add).then_inc(v_u, 1)
                dve.wait_ge(v_u, n * 2 + 2)
                assert c.n == Z_STEPS, c.n

            prepare(0)

            def image(i, more):
                c = Steps(dve, d_prep, i * DVE_PREPS)
                V.memset(acc, 0.0).then_inc(acc_zero, 1)
                t0 = i * STRIPS

                def build(b, k, loads, t):
                    dve.wait_ge(x_loaded[k], loads * 48)
                    dve.wait_ge(mixed, t - 1 + MIXED_CREDIT)
                    fg = lambda a: a.rearrange("p a o -> p (a o)")
                    for g in range(2):
                        b.did(V.scalar_tensor_tensor(fg(wst[:, k % 2, g]), fg(mix_s[:, 1, g]), strip[:, k, P + 2 * g:P + 2 * g + 1], fg(mix_s[:, 0, g]), ALU.mult, ALU.add))
                    b.settle()
                    b.did(V.scalar_tensor_tensor(fg(wst[:, k % 2, 0]), fg(mix_s[:, 2, 0]), strip[:, k, P + 1:P + 2], fg(wst[:, k % 2, 0]), ALU.mult, ALU.add))
                    V.scalar_tensor_tensor(fg(wst[:, k % 2, 1]), fg(mix_s[:, 2, 1]), strip[:, k, P + 3:P + 4], fg(wst[:, k % 2, 1]), ALU.mult, ALU.add).then_inc(w_ready, 1)

                def row_sums(b, k, t):
                    dve.wait_ge(g_taken, t + 1)
                    dve.wait_ge(g_ready, t + FREE)
                    b.then(V.scalar_tensor_tensor(gt[:], fix[:], v1(0), gp[:, 0, :], ALU.mult, ALU.add))
                    o = k % 2
                    gx, gh = slice(0, 12), slice(12, 24)
                    b.did(V.tensor_tensor(gst[0:HP, o, 0, :], gt[HP:P, gx], gp[HP:P, 1, gx], ALU.add))
                    b.did(V.tensor_tensor(gst[HP:P, o, 0, :], gt[HP:P, gh], gp[HP:P, 1, gh], ALU.add))
                    b.did(V.tensor_tensor(gst[0:HP, o, 1, :], gt[0:HP, gh], gp[0:HP, 1, gh], ALU.add))
                    V.tensor_tensor(gst[HP:P, o, 1, :], gt[0:HP, gx], gp[0:HP, 1, gx], ALU.add).then_inc(g_ready, 1)

                def combine(b, k, s, t):
                    o = k % 2
                    dve.wait_ge(e_done, t + 1)
                    b.then(V.tensor_copy(ev_e[:, o, :], ps[:, BE, 0:6]))
                    dve.wait_ge(y_done, t + FREE)
                    for a, done, dst in ((AXB, pc_done, vc), (AXC, ps_done, vs)):
                        dve.wait_ge(done, t + 1)
                        for q in range(2):
                            w = slice(HALF * q, HALF * (q + 1))
                            b.did(V.scalar_tensor_tensor(dst[:, w], ps[:, BP + a, w], ev_e[:, o, 2 * a + q:2 * a + q + 1], trig[:, a, w], ALU.add, ALU.mult))
                    b.settle()
                    dve.wait_ge(mixed, t + 1 + MIXED_CREDIT)
                    for q in range(2):
                        w = slice(HALF * q, HALF * (q + 1))
                        b.did(V.scalar_tensor_tensor(vy[:, w], ps[:, BP + AXS, w], ev_e[:, o, 4 + q:5 + q], vc[:, w], ALU.add, ALU.add))
                    b.settle()
                    V.scalar_tensor_tensor(x1[:, bass.ds(s, 1), :].rearrange("p a w -> p (a w)"), vs, v1(0), vy,
                                           ALU.add, ALU.add, accum_out=red[:, k:k + 1]).then_inc(y_done, 1)
                    dve.wait_ge(y_done, t + 1 + FREE)
                    b.did(V.tensor_copy(cols[:, 0, bass.ds(s, 1)], red[:, k:k + 1]))

                u0 = i * (STRIPS // UNROLL)
                b = Steps(dve, b_steps, i * (STRIPS * DVE_B))
                build(b, 0, u0 + 1, t0)
                row_sums(b, 0, t0)
                assert b.n == 7
                with dve.Fori(0, STRIPS // UNROLL - 1) as j:
                    for k in range(UNROLL):
                        s = j * UNROLL + k
                        b = Steps(dve, b_steps, (t0 + s) * DVE_B + 7)
                        build(b, (k + 1) % UNROLL, u0 + j + 1 + (k + 1) // UNROLL, t0 + s + 1)
                        combine(b, k, s, t0 + s)
                        row_sums(b, (k + 1) % UNROLL, t0 + s + 1)
                        assert b.n == DVE_B, b.n
                for s in range(STRIPS - UNROLL, STRIPS):
                    b = Steps(dve, b_steps, (t0 + s) * DVE_B + 7)
                    if s + 1 < STRIPS:
                        build(b, (s + 1) % UNROLL, u0 + s // UNROLL + 1, t0 + s + 1)
                    combine(b, s % UNROLL, s, t0 + s)
                    if s + 1 < STRIPS:
                        row_sums(b, (s + 1) % UNROLL, t0 + s + 1)
                assert b.n == DVE_B - 7

                dve.wait_ge(y_done, t0 + STRIPS + FREE)
                dve.wait_ge(y_squared, t0 + STRIPS + FREE)
                b.settle()
                c.did(V.tensor_reduce(v1(ST1), cols[:, 0, 0:STRIPS], AX_X, ALU.add))
                V.tensor_reduce(v1(ST1 + 1), cols[:, 1, 0:STRIPS], AX_X, ALU.add).then_inc(v_sums1, 1)
                dve.wait_ge(p_stat1, i + 1)
                c.then(V.tensor_scalar(v1(MEANP), stat[:, 2:3], float(-N), None, ALU.mult))
                V.tensor_scalar(colv, ps[:, BT, :], v1(MEANP), None, ALU.add).then_inc(v_colv, 1)
                variance(c, stat[:, 0:2], 0)
                dve.wait_ge(v_colv, i + 1)
                c.did(V.tensor_reduce(v1(SV), colv, AX_X, ALU.add))
                if more:
                    take_next(i + 1)
                with dve.Fori(0, STRIPS // DOTS) as j:
                    g0 = i * (STRIPS // DOTS) + j
                    dve.wait_ge(dots_kept, g0 + FREE)
                    for k in range(DVE_DOTS):
                        dve.wait_ge(dotted, g0 * DVE_DOTS + k - 1 + DOT_CREDIT)
                        V.scalar_tensor_tensor((vc, vy)[k % 2], x1[:, bass.ds(j * DOTS + k, 1), :].rearrange("p a w -> p (a w)"), 1.0, colv,
                                               ALU.mult, ALU.mult, accum_out=red[:, k:k + 1]).then_inc(dotted, 1)
                    dve.wait_ge(dotted, g0 * DVE_DOTS + DVE_DOTS + DOT_CREDIT)
                    V.tensor_copy(cols[:, 2, bass.ds(j * DOTS, DVE_DOTS)], red[:, 0:DVE_DOTS]).then_inc(dots_kept, 1)
                dve.wait_ge(dots_kept, (i + 1) * (STRIPS // DOTS) + FREE)
                dve.wait_ge(a_dotted, (i + 1) * (STRIPS // DOTS * OTHERS) + OTHERS)
                inverse_root(i, c, 2, 0)
                c.settle()
                S, Q, D, GA, A_, B_, T1, T2 = (cols[:, k, 0:STRIPS] for k in range(8))
                c.then(V.tensor_tensor(v1(SV), v1(SV), v1(0), ALU.mult))
                c.then(V.tensor_scalar(GA, D, v1(SV), 0.0, ALU.subtract, ALU.is_gt))
                c.then(V.tensor_scalar(GA, GA, v1(1), None, ALU.mult))
                c.did(V.tensor_scalar(A_, GA, 1.0, None, ALU.add))
                c.then(V.tensor_scalar(B_, GA, v1(2), None, ALU.mult))
                c.did(V.tensor_tensor(T1, A_, S, ALU.mult))
                c.then(V.tensor_tensor(T2, A_, Q, ALU.mult))
                c.did(V.tensor_tensor(T2, T2, A_, ALU.mult))
                c.then(V.tensor_scalar(GA, B_, float(N), None, ALU.mult))
                c.then(V.scalar_tensor_tensor(D, T1, 2.0, GA, ALU.mult, ALU.add))
                c.did(V.tensor_tensor(D, D, B_, ALU.mult))
                c.then(V.tensor_tensor(T1, T1, GA, ALU.add))
                c.then(V.tensor_tensor(T2, T2, D, ALU.add))
                c.did(V.tensor_reduce(v1(ST), T1, AX_X, ALU.add))
                V.tensor_reduce(v1(ST + 1), T2, AX_X, ALU.add).then_inc(v_sums2, 1)
                for e in (0, HALF + 1):
                    c.did(V.memset(cin[:, :, :, e:e + 1], 0.0))
                dve.wait_ge(p_stat2, i + 1)
                c.then(V.tensor_copy(v1(MEANP), stat[:, 0:1]))
                V.tensor_scalar(B_, B_, v1(MEANP), None, ALU.subtract).then_inc(v_gates, 1)
                moments(i, c, 3, stat[:, 0:2], ZV)

                def conv_weights(pad, layer, done):
                    for e in (0, HALF + 1) if pad is not None else ():
                        any_ = trig[:, 0, 0:SLOTS * TILES].rearrange("p (k t w) -> p k t w", k=SLOTS, t=TILES)
                        c.did(V.tensor_scalar(cin[:, 0:SLOTS, :, e:e + 1], any_, 0.0, pad, ALU.mult, ALU.add))
                    flat_c = lambda a: a.rearrange("p m o -> p (m o)")
                    V.scalar_tensor_tensor(flat_c(conv_s[:]), flat_c(conv_w[:, layer]), v1(ZV + 1),
                                           flat_c(conv_eye[:, layer]), ALU.mult, ALU.add).then_inc(done, 1)

                conv_weights(None, 0, v_conv2)
                def squares(j):
                    dve.wait_ge(c_reduced, u0 + j + FREE)
                    for k in range(UNROLL):
                        s = j * UNROLL + k
                        n = i * STRIPS + s
                        dve.wait_ge(evicted, i * (2 * STRIPS) + s + 1 + CONV_CREDIT)
                        dve.wait_ge(c_squared, n + CONV_CREDIT - 1)
                        V.scalar_tensor_tensor((vc, vs)[k % 2], cout[:, k % COUTS, :], 1.0, cout[:, k % COUTS, :], ALU.mult, ALU.mult,
                                               accum_out=red[:, k:k + 1]).then_inc(c_squared, 1)
                    dve.wait_ge(c_squared, i * STRIPS + j * UNROLL + UNROLL + CONV_CREDIT)
                    V.tensor_copy(cols[:, 3, bass.ds(j * UNROLL, UNROLL)], red[:, 0:UNROLL]).then_inc(c_reduced, 1)

                squares(0)
                for e, uses in ((0, 2), (1, 1)):
                    dve.wait_ge(d_loaded[e], (i * USES[e] + uses) * (8 * 16))
                    dve.wait_ge(e_loaded[e], (i * USES[e] + uses) * (4 * 16))
                c.did(V.memset(RING[2][:, :, :, 0:1], 0.0))
                c.then(V.memset(RING[2][:, :, :, HALF + 1:HALF + 2], 0.0))
                dve.sem_inc(third_ready, 1)
                with dve.Fori(1, STRIPS // UNROLL) as j:
                    squares(j)
                dve.sem_inc(third_ready, 2 * STRIPS - 1)
                dve.wait_ge(c_reduced, u0 + STRIPS // UNROLL + FREE)
                for q in (2, 3):
                    V.tensor_reduce(v1(ST + q - 2), cols[:, q, :], AX_X, ALU.add).then_inc(v_sums3, 1)
                dve.wait_ge(p_stat3, i + 1)
                c.then(V.tensor_copy(v1(CM), stat[:, 2:3]))
                V.tensor_scalar(vc[0:C, :], trig[0:C, 0, :], 0.0, v1(CM, 0, C), ALU.mult, ALU.add).then_inc(v_pad3, 1)
                moments(i, c, 4, stat[:, 0:2], ZV)
                conv_weights(v1(ZV), 1, v_conv3)
                dve.wait_ge(p_bias3, i + 1)
                V.tensor_tensor(v1(BIAS3), v1(CM), stat[:, 4:5], ALU.subtract).then_inc(v_bias3, 1)
                assert c.n == DVE_PREPS, c.n
                if more:
                    prepare(i + 1)

            with dve.Fori(0, B - 1) as i:
                image(i, True)
            image(B - 1, False)

        @block.tensor
        def _(pe):
            pe.sem_inc(a_projected, A_CREDIT)
            pe.sem_inc(mixed, MIXED_CREDIT)
            pe.sem_inc(convolved, CONV_CREDIT)
            pe.sem_inc(h_done, FREE)
            pe.wait_ge(s_const, 16 * 16)

            def chunk(k):
                return lambda a: a.rearrange("p (h w q) -> p q h w", h=2, q=2)[:, k // 2, k % 2]

            def statistics(rng, sums, dst, tab, n):
                return pe.matmul(dst, tab[0:n, rng[0]:rng[1]], sums, start=True, stop=True)

            def project(k, first):
                for e in range(2):
                    mm = pe.matmul(ps[HP * e:HP * (e + 1), BZ, :], strip[:, k + e, P + 4:P + 4 + HP], xa[:, k + e, :],
                                   start=first, stop=False, skip_group_check=True)
                mm.then_inc(a_projected, 2)

            def project_first(k, j, first):
                for slot in (k, k + 1):
                    pe.wait_ge(a_loaded[slot], j * 16 + 16)
                    pe.wait_ge(a_table[slot], j * 16 + 16)
                project(k, first)

            for k in range(0, UNROLL, 2):
                project_first(k, 0, k == 0)
            with pe.Fori(1, STRIPS // UNROLL) as j:
                for k in range(0, UNROLL, 2):
                    project_first(k, j, False)

            def prepare_z(n):
                pe.wait_ge(a_kept, n + 1)
                if type(n) is not int:
                    pe.wait_ge(v_bias3, n)
                for k in range(4):
                    mm = pe.matmul(ps[:, BZ, ZR * k:ZR * (k + 1)], zz[:, k * P:(k + 1) * P], fold[:], start=True, stop=True)
                mm.then_inc(p_zt, 1)
                pe.matmul(ps[0:ZR, BT, :], fold[:], zz[:], start=True, stop=True).then_inc(p_zin, 1)

            def prepare_h(n):
                pe.wait_ge(v_zt, n + 1)
                for cols_to, cols_of in ((lambda o: ps[0:ZR, BH, HALF * o:HALF * (o + 1)], slice(0, HALF)),
                                         (lambda o: ps[0:ZR, BZ, NG * o:NG * (o + 1)], slice(HALF, HW_))):
                    for k in range(4):
                        mm = pe.matmul(cols_to(int(k < 2)), zt[:, k, :], hil[:, k, cols_of], start=(k % 2 == 0), stop=(k % 2 == 1))
                mm.then_inc(p_zh, 1)
                pe.wait_ge(v_sums0, n + 1)
                pe.wait_ge(v_xsq, n + 1)
                pe.matmul(stat[:, 0:1], zsel[:, 0:P], vec[0:ZR, ZSUM:ZSUM + 1], start=True, stop=True)
                pe.matmul(stat[0:ZR, 2:3], zsel[:, P:P + ZR], vec[0:ZR, ZSUM:ZSUM + 1], start=True, stop=True)
                statistics(G_OUT, vec[:, XSQ:XSQ + 1], stat[:, 1:2], gsel, P)
                statistics(G_Z, vec[:, XSQ:XSQ + 1], stat[0:ZR, 3:4], gsel, P).then_inc(p_stat, 1)

            def prepare_u(n):
                pe.wait_ge(v_z, n + 1)
                for a in range(3):
                    pe.matmul(ps[0:48, BU[a], :], u_base[:, 2 * a, :], vc[0:ZR, :], start=True, stop=False)
                    pe.matmul(ps[0:48, BU[a], :], u_base[:, 2 * a + 1, :], vs[0:ZR, :], start=False, stop=True)
                for e, (k, g0) in enumerate(((0, 0), (1, 12), (2, 6), (3, 18))):
                    mm = pe.matmul(ps[0:48, BE, 0:6], u_base[:, k, :], gt[0:ZR, g0:g0 + 6], start=(e == 0), stop=(e == 3))
                mm.then_inc(p_u, 1)

            pe.wait_ge(s_based, 1)
            prepare_z(0)
            prepare_h(0)
            prepare_u(0)

            def image(i, more):
                t0 = i * STRIPS
                u0 = i * (STRIPS // UNROLL)

                def turn(k, loads, t):
                    pe.wait_ge(x_loaded[k], loads * 48)
                    pe.wait_ge(xt_ready, t + FREE)
                    for q in range(4):
                        mm = pe.transpose(ps[:, BT, q * P:(q + 1) * P], chunk(q)(xin[:, k, :]), eye[:])
                    mm.then_inc(turned, 1)

                def hilbert(t):
                    pe.wait_ge(xt_ready, t + 1 + FREE)
                    pe.wait_ge(h_ready, t * 2 + FREE)
                    for q in range(4):
                        mm = pe.matmul(ps[:, BH + (q < 2), 0:HW_], xt[:, q, :], hil[:, q, :], start=(q % 2 == 0), stop=(q % 2 == 1))
                    mm.then_inc(h_done, 1)

                def mix(k, t):
                    o = k % 2
                    pe.wait_ge(y_done, t + FREE)
                    pe.matmul(ps[:, BP + AXS, :], strip[:, k, 0:P], u[:], start=True, stop=False)

                    def product(a, start, done):
                        for g in range(2):
                            mm = pe.matmul(ps[HP * g:HP * g + HP, BP + a, :], wst[:, o, g, a, :], stack[:, o, g, :], start=start, stop=True)
                        mm.then_inc(done, 1)

                    pe.wait_ge(w_ready, t + 1)
                    pe.wait_ge(h_ready, t * 2 + 2 + FREE)
                    product(AXB, True, pc_done)
                    pe.wait_ge(g_ready, t + 1 + FREE)
                    for g in range(2):
                        for a in range(2):
                            mm = pe.matmul(ps[HP * g:HP * g + HP, BE, 0:6], wst[:, o, g, a, :], gst[:, o, g, 6 * a:6 * a + 6], start=(a == 0), stop=(a == 1))
                    mm.then_inc(e_done, 1)
                    product(AXC, True, ps_done)
                    product(AXS, False, mixed)

                pe.wait_ge(v_u, i * 2 + 2)
                pe.wait_ge(evicted, i * (2 * STRIPS) + CONV_CREDIT)
                turn(0, u0 + 1, t0)
                hilbert(t0)
                def project_next(s, uses, k):
                    if more and k % 2:
                        for slot in (k - 1, k):
                            pe.wait_ge(a_loaded[slot], (u0 + STRIPS // UNROLL + uses + 1) * 16)
                        project(k - 1, first=type(s) is int and s == 1)

                def step(s, uses, k):
                    turn((k + 1) % UNROLL, u0 + uses + 1 + (k + 1) // UNROLL, t0 + s + 1)
                    project_next(s, uses, k)
                    mix(k, t0 + s)
                    hilbert(t0 + s + 1)

                for s in range(UNROLL):
                    step(s, 0, s)
                with pe.Fori(1, STRIPS // UNROLL - 1) as j:
                    for k in range(UNROLL):
                        step(j * UNROLL + k, j, k)
                for s in range(STRIPS - UNROLL, STRIPS):
                    if s + 1 < STRIPS:
                        turn((s + 1) % UNROLL, u0 + s // UNROLL + 1, t0 + s + 1)
                    project_next(s, s // UNROLL, s % UNROLL)
                    mix(s % UNROLL, t0 + s)
                    if s + 1 < STRIPS:
                        hilbert(t0 + s + 1)

                pe.wait_ge(v_sums1, i + 1)
                pe.wait_ge(y_added, t0 + STRIPS + FREE)
                statistics(G_OUT, vec[:, ST1:ST1 + 2], stat[:, 0:2], gsel, P)
                statistics(G_PART, vec[:, ST1:ST1 + 2], stat[:, 2:4], gsel, P)
                pe.matmul(ps[:, BT, :], partner[:], acc, start=True, stop=True).then_inc(p_stat1, 1)
                pe.wait_ge(v_sums2, i + 1)
                statistics(G_OUT, vec[:, ST:ST + 2], stat[:, 0:2], gsel, P).then_inc(p_stat2, 1)

                def conv(n, k, strip_in):
                    pe.wait_ge(evicted, n + 1 - 4 + CONV_CREDIT)
                    for m, (q, first) in enumerate(((0, 0), (0, 1), (1, 1), (1, 2))):
                        for t in range(TILES):
                            mm = pe.matmul(ps[TM * t:TM * (t + 1), 2 + k, HALF * q:HALF * (q + 1)], conv_s[:, m, :],
                                           strip_in[:, t, first:first + HALF], start=(m % 2 == 0), stop=(m % 2 == 1))
                    mm.then_inc(convolved, 1)

                def conv_group(g, e, use):
                    for k in range(UNROLL):
                        pe.wait_ge(v_conv2, i + 1)
                        pe.wait_ge(d_loaded[e], (i * USES[e] + use + 1) * (8 * 16))
                        pe.wait_ge(e_loaded[e], (i * USES[e] + use + 1) * (4 * 16))
                        pe.wait_ge(d_top, (i + 1) * 32)
                        if type(g) is int and g == GROUPS - 1:
                            pe.wait_ge(d_bottom, (i + 1) * 32)
                        conv(i * (2 * STRIPS) + g * UNROLL + k, k, RING[e][:, k])

                in_groups(pe, conv_group)
                pe.wait_ge(v_sums3, i * 2 + 2)
                statistics(G_CIN, vec[:, ST:ST + 2], stat[:, 0:2], gsel, P)
                statistics(G_OUT, vec[:, ST:ST + 2], stat[:, 2:4], gsel, P).then_inc(p_stat3, 1)
                pe.wait_ge(v_conv3, i + 1)
                for t in range(TILES):
                    for m in range(2):
                        mm = pe.matmul(stat[TM * t:TM * (t + 1), 4:5], conv_s[:, m, :], vec[:, ZV:ZV + 1], start=(m == 0), stop=(m == 1))
                mm.then_inc(p_bias3, 1)
                done = 0
                for upto, also in ((4, prepare_z), (8, prepare_h), (12, prepare_u), (STRIPS // UNROLL, None)):
                    with pe.Fori(done, upto) as j:
                        for k in range(UNROLL):
                            pe.wait_ge(c_loaded[k], (i * (STRIPS // UNROLL) + j + 1) * 32)
                            conv((i * 2 + 1) * STRIPS + j * UNROLL + k, k, cin[:, k])
                    done = upto
                    if also and more:
                        also(i + 1)

            with pe.Fori(0, B - 1) as i:
                image(i, True)
            image(B - 1, False)


def kernel(x, L0_conv_w_real, L0_conv_w_imag, L0_conv_b_real, L0_conv_b_imag, L2_conv_W, L3_conv_weight):
    import numpy as _np
    import concourse.bacc as _bacc
    from concourse import mybir as _mybir
    from concourse.bass_utils import run_bass_kernel_spmd as _run

    a = [_np.asarray(v) for v in (L0_conv_w_real, L0_conv_w_imag, L0_conv_b_real, L0_conv_b_imag, L2_conv_W, L3_conv_weight)]
    arrays = {"x": _np.ascontiguousarray(x)}
    arrays.update(tables())
    arrays.update(placed(*a))
    nc = _bacc.Bacc("TRN2", target_bir_lowering=False, num_devices=1)
    args = {n: nc.dram_tensor(n, v.shape, _mybir.dt.from_np(v.dtype), kind="ExternalInput").ap() for n, v in arrays.items()}
    args["out"] = nc.dram_tensor("out", (B, C, N, N), _mybir.dt.float32, kind="ExternalOutput").ap()
    program(nc, **args)
    r = _run(nc, [arrays], core_ids=[0])
    return r.results[0]["out"]
```
